# Optimizing a Trainium2 kernel written in Bass

```python
import numpy as np
import jax
import jax.numpy as jnp

def _softmax(x, axis=-1):
    return jax.nn.softmax(x, axis=axis)

def _gelu(x):
    return jax.nn.gelu(x, approximate=True)

def _silu(x):
    return jax.nn.silu(x)

def _sigmoid(x):
    return jax.nn.sigmoid(x)

def _layernorm(x, axis=-1, eps=1e-05):
    m = jnp.mean(x, axis=axis, keepdims=True)
    v = jnp.var(x, axis=axis, keepdims=True)
    return (x - m) / jnp.sqrt(v + eps)

def _scatter_add(tgt, idx, src, axis=0):
    return tgt.at[idx].add(src)

def _segment_sum(src, seg, n):
    return jax.ops.segment_sum(src, seg, n)
kernel_name = 'mk_adaln_d1_jaxref_r8_5cd684'

def setup_inputs(seed: int=0):
    np.random.seed(seed)
    _w = jnp.asarray

    def _L0_attn_setup():
        import jax, jax.numpy as jnp
        import numpy as np
        D_MODEL = 128
        HEAD_DIM = 32
        MEMORY_SIZE = 64
        SPARSITY_RATIO = 0.1
        NEG_INF = -1000000000.0

        def _full_attention(x, qkv_w, scale):
            qkv = x @ qkv_w
            q, k, v = jnp.split(qkv, 3, axis=-1)
            scores = jnp.einsum('bsh,bth->bst', q, k) * scale
            probs = jax.nn.softmax(scores, axis=-1)
            return probs @ v

        def _sparse_global_attention(x, qkv_w, scale):
            qkv = x @ qkv_w
            q, k, v = jnp.split(qkv, 3, axis=-1)
            scores = jnp.einsum('bsh,bth->bst', q, k) * scale
            seq_len = x.shape[1]
            k_sparse = max(1, int(seq_len * SPARSITY_RATIO))
            topk_vals, _ = jax.lax.top_k(scores, k_sparse)
            kth = topk_vals[..., -1:]
            masked = jnp.where(scores >= kth, scores, NEG_INF)
            probs = jax.nn.softmax(masked, axis=-1)
            return probs @ v

        def _memory_head(x, memory_bank, memory_proj_w, mem_out_w, mem_out_b):
            x_proj = x @ memory_proj_w
            mem_scores = jnp.einsum('bsh,mh->bsm', x_proj, memory_bank)
            mem_weights = jax.nn.softmax(mem_scores, axis=-1)
            retrieved = jnp.einsum('bsm,mh->bsh', mem_weights, memory_bank)
            combined = jnp.concatenate([x_proj, retrieved], axis=-1)
            return combined @ mem_out_w + mem_out_b

        def _prediction_head(x, pred_in_w, pred_in_b, pred1_w, pred1_b, pred2_w, pred2_b):
            h = x @ pred_in_w + pred_in_b
            h = h @ pred1_w + pred1_b
            h = jax.nn.gelu(h, approximate=False)
            return h @ pred2_w + pred2_b
        key = jax.random.key(seed)
        ks = jax.random.split(key, 16)
        s = lambda fan_in: 1.0 / np.sqrt(fan_in)
        inp = {'x': jax.random.normal(ks[0], (2, 512, D_MODEL), dtype=jnp.float32), 'local_qkv_w': jax.random.uniform(ks[1], (D_MODEL, 3 * HEAD_DIM), minval=-s(D_MODEL), maxval=s(D_MODEL)), 'sparse_qkv_w': jax.random.uniform(ks[2], (D_MODEL, 3 * HEAD_DIM), minval=-s(D_MODEL), maxval=s(D_MODEL)), 'memory_bank': jax.random.normal(ks[3], (MEMORY_SIZE, HEAD_DIM), dtype=jnp.float32), 'memory_proj_w': jax.random.uniform(ks[4], (D_MODEL, HEAD_DIM), minval=-s(D_MODEL), maxval=s(D_MODEL)), 'mem_out_w': jax.random.uniform(ks[5], (2 * HEAD_DIM, HEAD_DIM), minval=-s(2 * HEAD_DIM), maxval=s(2 * HEAD_DIM)), 'mem_out_b': jax.random.uniform(ks[6], (HEAD_DIM,), minval=-s(2 * HEAD_DIM), maxval=s(2 * HEAD_DIM)), 'pred_in_w': jax.random.uniform(ks[7], (D_MODEL, HEAD_DIM), minval=-s(D_MODEL), maxval=s(D_MODEL)), 'pred_in_b': jax.random.uniform(ks[8], (HEAD_DIM,), minval=-s(D_MODEL), maxval=s(D_MODEL)), 'pred1_w': jax.random.uniform(ks[9], (HEAD_DIM, 2 * HEAD_DIM), minval=-s(HEAD_DIM), maxval=s(HEAD_DIM)), 'pred1_b': jax.random.uniform(ks[10], (2 * HEAD_DIM,), minval=-s(HEAD_DIM), maxval=s(HEAD_DIM)), 'pred2_w': jax.random.uniform(ks[11], (2 * HEAD_DIM, HEAD_DIM), minval=-s(2 * HEAD_DIM), maxval=s(2 * HEAD_DIM)), 'pred2_b': jax.random.uniform(ks[12], (HEAD_DIM,), minval=-s(2 * HEAD_DIM), maxval=s(2 * HEAD_DIM)), 'warboss_w': jax.random.uniform(ks[13], (4 * HEAD_DIM, D_MODEL), minval=-s(4 * HEAD_DIM), maxval=s(4 * HEAD_DIM)), 'warboss_b': jax.random.uniform(ks[14], (D_MODEL,), minval=-s(4 * HEAD_DIM), maxval=s(4 * HEAD_DIM))}
        return inp
    _L0_attn_in = _L0_attn_setup()

    def _L0_ffn_setup():
        import jax, jax.numpy as jnp
        import numpy as np
        B, S, D, F, E, NS, K = (2, 128, 128, 512, 8, 8, 2)
        FS = F // NS
        key = jax.random.key(seed)
        ks = jax.random.split(key, 8)
        scale = 0.02
        return {'hidden_states': jax.random.normal(ks[0], (B, S, D), jnp.float32), 'gate_W': jax.random.normal(ks[1], (E, D), jnp.float32) * scale, 'w1_e': jax.random.normal(ks[2], (E, D, F), jnp.float32) * scale, 'w3_e': jax.random.normal(ks[3], (E, D, F), jnp.float32) * scale, 'w2_e': jax.random.normal(ks[4], (E, F, D), jnp.float32) * scale, 'w1_s': jax.random.normal(ks[5], (NS, D, FS), jnp.float32) * scale, 'w3_s': jax.random.normal(ks[6], (NS, D, FS), jnp.float32) * scale, 'w2_s': jax.random.normal(ks[7], (NS, FS, D), jnp.float32) * scale}
    _L0_ffn_in = _L0_ffn_setup()
    _L0_c = _w((lambda *s: np.random.randn(*s).astype(np.float32) * 0.05)(2, 128))
    _L0_wmod = _w((lambda *s: np.random.randn(*s).astype(np.float32) * 0.05)(128, 6 * 128) * 128 ** (-0.5))
    _d = {'L0_attn_x': _L0_attn_in['x'], 'L0_attn_local_qkv_w': _L0_attn_in['local_qkv_w'], 'L0_attn_sparse_qkv_w': _L0_attn_in['sparse_qkv_w'], 'L0_attn_memory_bank': _L0_attn_in['memory_bank'], 'L0_attn_memory_proj_w': _L0_attn_in['memory_proj_w'], 'L0_attn_mem_out_w': _L0_attn_in['mem_out_w'], 'L0_attn_mem_out_b': _L0_attn_in['mem_out_b'], 'L0_attn_pred_in_w': _L0_attn_in['pred_in_w'], 'L0_attn_pred_in_b': _L0_attn_in['pred_in_b'], 'L0_attn_pred1_w': _L0_attn_in['pred1_w'], 'L0_attn_pred1_b': _L0_attn_in['pred1_b'], 'L0_attn_pred2_w': _L0_attn_in['pred2_w'], 'L0_attn_pred2_b': _L0_attn_in['pred2_b'], 'L0_attn_warboss_w': _L0_attn_in['warboss_w'], 'L0_attn_warboss_b': _L0_attn_in['warboss_b'], 'L0_ffn_gate_W': _L0_ffn_in['gate_W'], 'L0_ffn_w1_e': _L0_ffn_in['w1_e'], 'L0_ffn_w3_e': _L0_ffn_in['w3_e'], 'L0_ffn_w2_e': _L0_ffn_in['w2_e'], 'L0_ffn_w1_s': _L0_ffn_in['w1_s'], 'L0_ffn_w3_s': _L0_ffn_in['w3_s'], 'L0_ffn_w2_s': _L0_ffn_in['w2_s'], 'L0_c': _L0_c, 'L0_wmod': _L0_wmod}
    _x0 = _d['L0_attn_x']
    _d['L0_attn_x'] = jax.random.normal(jax.random.fold_in(jax.random.key(seed), 1), (2, 1024, 128), dtype=_x0.dtype)
    del _x0
    return _d

def reference(L0_attn_x, L0_attn_local_qkv_w, L0_attn_sparse_qkv_w, L0_attn_memory_bank, L0_attn_memory_proj_w, L0_attn_mem_out_w, L0_attn_mem_out_b, L0_attn_pred_in_w, L0_attn_pred_in_b, L0_attn_pred1_w, L0_attn_pred1_b, L0_attn_pred2_w, L0_attn_pred2_b, L0_attn_warboss_w, L0_attn_warboss_b, L0_ffn_gate_W, L0_ffn_w1_e, L0_ffn_w3_e, L0_ffn_w2_e, L0_ffn_w1_s, L0_ffn_w3_s, L0_ffn_w2_s, L0_c, L0_wmod):

    def _L0_attn_ref(x, local_qkv_w, sparse_qkv_w, memory_bank, memory_proj_w, mem_out_w, mem_out_b, pred_in_w, pred_in_b, pred1_w, pred1_b, pred2_w, pred2_b, warboss_w, warboss_b):
        import jax, jax.numpy as jnp
        import numpy as np
        D_MODEL = 128
        HEAD_DIM = 32
        MEMORY_SIZE = 64
        SPARSITY_RATIO = 0.1
        NEG_INF = -1000000000.0

        def _full_attention(x, qkv_w, scale):
            qkv = x @ qkv_w
            q, k, v = jnp.split(qkv, 3, axis=-1)
            scores = jnp.einsum('bsh,bth->bst', q, k) * scale
            probs = jax.nn.softmax(scores, axis=-1)
            return probs @ v

        def _sparse_global_attention(x, qkv_w, scale):
            qkv = x @ qkv_w
            q, k, v = jnp.split(qkv, 3, axis=-1)
            scores = jnp.einsum('bsh,bth->bst', q, k) * scale
            seq_len = x.shape[1]
            k_sparse = max(1, int(seq_len * SPARSITY_RATIO))
            topk_vals, _ = jax.lax.top_k(scores, k_sparse)
            kth = topk_vals[..., -1:]
            masked = jnp.where(scores >= kth, scores, NEG_INF)
            probs = jax.nn.softmax(masked, axis=-1)
            return probs @ v

        def _memory_head(x, memory_bank, memory_proj_w, mem_out_w, mem_out_b):
            x_proj = x @ memory_proj_w
            mem_scores = jnp.einsum('bsh,mh->bsm', x_proj, memory_bank)
            mem_weights = jax.nn.softmax(mem_scores, axis=-1)
            retrieved = jnp.einsum('bsm,mh->bsh', mem_weights, memory_bank)
            combined = jnp.concatenate([x_proj, retrieved], axis=-1)
            return combined @ mem_out_w + mem_out_b

        def _prediction_head(x, pred_in_w, pred_in_b, pred1_w, pred1_b, pred2_w, pred2_b):
            h = x @ pred_in_w + pred_in_b
            h = h @ pred1_w + pred1_b
            h = jax.nn.gelu(h, approximate=False)
            return h @ pred2_w + pred2_b
        scale = HEAD_DIM ** (-0.5)
        local_out = _full_attention(x, local_qkv_w, scale)
        sparse_out = _sparse_global_attention(x, sparse_qkv_w, scale)
        mem_out = _memory_head(x, memory_bank, memory_proj_w, mem_out_w, mem_out_b)
        pred_out = _prediction_head(x, pred_in_w, pred_in_b, pred1_w, pred1_b, pred2_w, pred2_b)
        combined = jnp.concatenate([local_out, sparse_out, mem_out, pred_out], axis=-1)
        return combined @ warboss_w + warboss_b

    def _L0_ffn_ref(hidden_states, gate_W, w1_e, w3_e, w2_e, w1_s, w3_s, w2_s):
        import jax, jax.numpy as jnp
        import numpy as np
        B, S, D, F, E, NS, K = (2, 128, 128, 512, 8, 8, 2)
        FS = F // NS
        b, s, d = hidden_states.shape
        e = gate_W.shape[0]
        flat = hidden_states.reshape(-1, d)
        T = flat.shape[0]
        logits = (flat @ gate_W.T).astype(jnp.float32)
        probs = jax.nn.softmax(logits, axis=-1)
        top_v, top_i = jax.lax.top_k(probs, K)
        gates = jnp.zeros((T, e), probs.dtype).at[jnp.arange(T)[:, None], top_i].set(top_v)
        g = jax.nn.silu(jnp.einsum('td,edf->etf', flat, w1_e))
        u = jnp.einsum('td,edf->etf', flat, w3_e)
        out_e = jnp.einsum('etf,efd->etd', g * u, w2_e)
        routed = jnp.einsum('te,etd->td', gates, out_e).reshape(b, s, d)
        gs = jax.nn.silu(jnp.einsum('bsd,ndf->nbsf', hidden_states, w1_s))
        us = jnp.einsum('bsd,ndf->nbsf', hidden_states, w3_s)
        shared = jnp.einsum('nbsf,nfd->bsd', gs * us, w2_s) / w1_s.shape[0]
        alpha = 0.5
        return alpha * shared + (1.0 - alpha) * routed
    x = L0_attn_x
    mod = (_silu(L0_c) @ L0_wmod).reshape(L0_c.shape[0], 6, 1, -1)
    sa, ca, ga, sb, cb, gb = (mod[:, 0], mod[:, 1], mod[:, 2], mod[:, 3], mod[:, 4], mod[:, 5])
    ga = (2 * (ga >= 0) - 1) * jnp.maximum(jnp.abs(ga), 0.25)
    gb = (2 * (gb >= 0) - 1) * jnp.maximum(jnp.abs(gb), 0.25)
    h = _layernorm(x, axis=-1) * (1 + ca) + sa
    x = x + ga * _L0_attn_ref(h, L0_attn_local_qkv_w, L0_attn_sparse_qkv_w, L0_attn_memory_bank, L0_attn_memory_proj_w, L0_attn_mem_out_w, L0_attn_mem_out_b, L0_attn_pred_in_w, L0_attn_pred_in_b, L0_attn_pred1_w, L0_attn_pred1_b, L0_attn_pred2_w, L0_attn_pred2_b, L0_attn_warboss_w, L0_attn_warboss_b)
    h = _layernorm(x, axis=-1) * (1 + cb) + sb
    x = x + gb * _L0_ffn_ref(h, L0_ffn_gate_W, L0_ffn_w1_e, L0_ffn_w3_e, L0_ffn_w2_e, L0_ffn_w1_s, L0_ffn_w3_s, L0_ffn_w2_s)
    return x

_drawn_inputs = setup_inputs


def setup_inputs(seed=0):
    import zlib

    import numpy as np

    out = dict(_drawn_inputs(seed))
    spreads = {}
    factors = {'L0_attn_local_qkv_w': 8.0,
     'L0_attn_sparse_qkv_w': 7.29,
     'L0_attn_memory_bank': 3.263,
     'L0_attn_mem_out_b': 30.677,
     'L0_attn_pred_in_w': 7.217,
     'L0_attn_pred_in_b': 8.0,
     'L0_attn_pred1_w': 7.184,
     'L0_attn_pred1_b': 8.0,
     'L0_attn_pred2_w': 6.336,
     'L0_attn_pred2_b': 31.643,
     'L0_attn_warboss_b': 13.314,
     'L0_ffn_gate_W': 8.0,
     'L0_ffn_w1_e': 8.0,
     'L0_ffn_w3_e': 8.0,
     'L0_ffn_w2_e': 8.0,
     'L0_ffn_w1_s': 8.0,
     'L0_ffn_w3_s': 8.0,
     'L0_ffn_w2_s': 8.0}
    for name, (base, spread) in spreads.items():
        noise = np.random.default_rng([zlib.crc32(name.encode()), seed]).standard_normal(out[name].shape)
        drawn = base * np.exp(spread * noise) if base else spread * noise
        out[name] = jnp.asarray(drawn.astype(out[name].dtype))
    for name, factor in factors.items():
        out[name] = (out[name] * factor).astype(out[name].dtype)
    return out
```

```python
from contextlib import ExitStack

import concourse.bass as bass
from concourse import mybir

F32 = mybir.dt.float32
BF16 = mybir.dt.bfloat16
ALU = mybir.AluOpType
ACT = mybir.ActivationFunctionType
X = mybir.AxisListType.X

P = 128
NEG = -3.0e38


def build(nc, io):
    x_d, out_d = io["L0_attn_x"], io["out"]
    B, S, D = x_d.shape
    HD = io["L0_attn_memory_bank"].shape[1]
    MEM = io["L0_attn_memory_bank"].shape[0]
    E, _, F = io["L0_ffn_w1_e"].shape
    NS, _, FS = io["L0_ffn_w1_s"].shape
    NT = S // P
    TT = B * NT
    FC = F // P
    KTOP = max(1, int(S * 0.1))
    ROUNDS = (KTOP + 7) // 8
    SCALE = HD ** -0.5
    GRP = 512
    NG = S // GRP
    TG = GRP // P
    assert B == 2 and D == P and NS * FS == F and HD == 32 and MEM == 64 and E == NT

    ctx = ExitStack()
    with ctx:
        def sb(name, shape, dt=F32):
            return ctx.enter_context(nc.sbuf_tensor(name, shape, dt))

        def sem(name):
            return ctx.enter_context(nc.semaphore(name))

        ident = sb("ident", [P, P])
        ones = sb("ones", [P, P])
        earlier = sb("earlier", [P, E, E])
        cT = sb("cT", [P, B])
        sig = sb("sig", [P, 2, B])
        siluc = sb("siluc", [P, B])
        silub = sb("silub", [P, B, P])
        wmod = sb("wmod", [P, 6 * P])
        mcol = sb("mcol", [P, 4, B])
        gate_rows = sb("gate_rows", [P, 2, B, P])
        wq = sb("wq", [P, 2 * HD])
        wk = sb("wk", [P, 2 * HD])
        wrow = sb("wrow", [P, 2 * HD + MEM])
        proj = sb("proj", [P, HD])
        predin = sb("predin", [P, HD])
        bank = sb("bank", [MEM, HD])
        memout = sb("memout", [2 * HD, HD])
        pred2 = sb("pred2", [2 * HD, HD])
        gateW = sb("gateW", [E, P])
        gateWT = sb("gateWT", [P, E])
        pred1 = sb("pred1", [HD, 2 * HD])
        pred1b = sb("pred1b", [2 * HD, 1])
        bcols = sb("bcols", [HD, 3])
        bwide = sb("bwide", [HD, 2, P])
        wb = sb("wb", [P, P])
        wb_mem = sb("wb_mem", [HD, P])
        wb_pred = sb("wb_pred", [HD, P])
        wbias = sb("wbias", [P, P])
        turned = sb("turned", [P, 6, P])
        ab = sb("ab", [HD, 2, P])
        wp = sb("wp", [P, 2 * HD])
        bp = sb("bp", [2 * HD, 1])
        wcomb = sb("wcomb", [P, B, P])
        wx = sb("wx", [P, B, P])
        wpr = sb("wpr", [2 * HD, B, P])
        biasg = sb("biasg", [P, B, P])
        x_sb = sb("x_sb", [P, TT, P])
        x1 = sb("x1", [P, TT, P])
        stats = sb("stats", [P, TT, 6])
        mean = sb("mean", [P, TT])
        var = sb("var", [P, TT])
        sdev = sb("sdev", [P, TT])
        rstd = sb("rstd", [P, TT])
        lt = sb("lt", [P, 2, TT])
        xh = sb("xh", [P, 2, P])
        hs = sb("hs", [P, 2, P])
        qk = sb("qk", [2 * HD, TT, 2, P])
        gelu = sb("gelu", [2 * HD, 2, P])
        v = sb("v", [P, TT, 2, HD + 1])
        om = sb("om", [P, TT, HD + MEM])
        mstat = sb("mstat", [P, 3, TT])
        qs = sb("qs", [2 * HD, 2, P])
        s_all = sb("s_all", [P, TT, S])
        smax = sb("smax", [P, TT])
        snmax = sb("snmax", [P, TT])
        thr = sb("thr", [P, TT])
        junk = sb("junk", [P, S], BF16)
        nml = sb("nml", [P, 2])
        el = sb("el", [P, 2, S])
        es = sb("es", [P, S])
        et = sb("et", [P, 3, NT, P])
        rl = sb("rl", [P, 2])
        rs = sb("rs", [P, 1])
        kwork = sb("kwork", [P, S])
        k8 = sb("k8", [P, 8])
        tick = sb("tick", [1, 1])
        gtmp, gabs = (kwork[:, h * S // 2:(h + 1) * S // 2].rearrange("p (k b d) -> p k b d", k=2, b=B) for h in range(2))
        cs = sb("cs", [P, P])
        csT = sb("csT", [P, P])
        h2T = sb("h2T", [P, S])
        lg = sb("lg", [P, NT, E])
        g1 = sb("g1", [P, NT])
        cmp1, cmp2 = (kwork[:, h * S // 2:(h + 1) * S // 2].rearrange("p (t e j) -> p t e j", t=NT, e=E) for h in range(2))
        rank = sb("rank", [P, NT, E])
        gates = sb("gates", [P, NT, E])
        w13 = sb("w13", [P, 2, 2, F])
        w2 = sb("w2", [P, 2, FC, P])
        w13s = sb("w13s", [P, 2, F])
        w2s = sb("w2s", [P, FC, P])
        silu = sb("silu", [P, 2, GRP])
        gu = [el[:, :, :].rearrange("p a (c t) -> p (a c) t", t=GRP),
              sb("gu1", [P, FC, GRP])]
        acc = sb("acc", [P, NT, P])

        pb = [ctx.enter_context(nc.psum_tensor(f"pb{n}", [P, 2, 512], F32)) for n in range(4)]

        def bank_of(n):
            return pb[n // 2][:, n % 2, :]

        names = """l_x l_wmod l_small l_w0 l_w1 l_ws cst zeroed acc0 c_exp c_silu m_ps modded
        tr_w tr_c fold_ps fold_c weights x1_0 ln_st ln_sd ln_rs
        a_xh a_tr a_hs a_pa a_qk a_gl a_pb a_ev mem_s mem_e mem_d
        b_qs b_sl b_sc b_nm b_se b_el b_pv b_rl b_no pt_tr pt_ev k_ch thr_r
        t_e t_p t_pv t_rs t_no t_cs t_ct t_cc t_xm t_x1
        t_st b_sn h_st h_sd h_rs h_xh h_tr h_hs h_cp h_lg g_sub g_exp g_ch gated
        f_up f_sg f_gu f_dn f_ac o_add out_done dve_step""".split()
        q = {n: sem(n) for n in names}
        l_w = [q["l_w0"], q["l_w1"]]

        x_v = x_d.rearrange("b (t p) d -> p (b t) d", p=P)
        out_v = out_d.rearrange("b (t p) d -> p (b t) d", p=P)
        w1_d, w3_d, w2_d = io["L0_ffn_w1_e"], io["L0_ffn_w3_e"], io["L0_ffn_w2_e"]

        def column(a):
            return a.rearrange("(a b) -> a b", b=1)

        wlo, wsp, wbo = io["L0_attn_local_qkv_w"], io["L0_attn_sparse_qkv_w"], io["L0_attn_warboss_w"]
        small = [(proj[:], io["L0_attn_memory_proj_w"]), (predin[:], io["L0_attn_pred_in_w"]),
                 (bank[:], io["L0_attn_memory_bank"]), (memout[:], io["L0_attn_mem_out_w"]),
                 (pred2[:], io["L0_attn_pred2_w"]), (gateW[:], io["L0_ffn_gate_W"]),
                 (pred1[:], io["L0_attn_pred1_w"])]
        for k, w in enumerate((wlo, wsp)):
            small += [(wq[:, HD * k:HD * k + HD], w[:, 0:HD]), (wk[:, HD * k:HD * k + HD], w[:, HD:2 * HD]),
                      (wrow[:, HD * k:HD * k + HD], w[:, 2 * HD:3 * HD])]
        small += [(wb[0:HD, :], wbo[0:HD, :]), (wb[3 * HD:4 * HD, :], wbo[HD:2 * HD, :]),
                  (wb_mem[:], wbo[2 * HD:3 * HD, :]), (wb_pred[:], wbo[3 * HD:4 * HD, :]),
                  (wbias[:], io["L0_attn_warboss_b"].partition_broadcast(P)),
                  (pred1b[:], column(io["L0_attn_pred1_b"])), (bcols[:, 0:1], column(io["L0_attn_mem_out_b"])),
                  (bcols[:, 1:2], column(io["L0_attn_pred2_b"])), (bcols[:, 2:3], column(io["L0_attn_pred_in_b"]))]
        small += [(cT[:, b:b + 1], column(io["L0_c"][b])) for b in range(B)]
        ALL_SMALL = 16 * len(small)

        def col(t, n):
            return t[:, n:n + 1] if isinstance(n, int) else t[:, bass.ds(n, 1)]

        turns = [(proj[:], HD), (predin[:], HD), (bank[:], HD), (memout[:], HD), (pred2[:], HD), (gateW[:], P)]

        block = ctx.enter_context(nc.Block())

        @block.sync
        def _(sp):
            for dst, src in small[-2:]:
                sp.dma_start(dst, src).then_inc(q["l_small"], 16)
            sp.dma_start(wmod[:], io["L0_wmod"]).then_inc(q["l_wmod"], 16)
            for b in range(B):
                sp.dma_start(x_sb[:, NT * b:NT * b + NT, :], x_v[:, NT * b:NT * b + NT, :]).then_inc(q["l_x"], 16)
            for dst, src in small[0:-2:2]:
                sp.dma_start(dst, src).then_inc(q["l_small"], 16)

            def load_expert(e, s):
                for j, w in enumerate((w1_d, w3_d)):
                    sp.dma_start(w13[:, s, j, :], w[e]).then_inc(l_w[s], 16)
                sp.dma_start(w2[:, s, :, :], w2_d[e].rearrange("(c p) d -> p c d", p=P)).then_inc(l_w[s], 16)

            for s in range(2):
                load_expert(s, s)
            for j, w in enumerate((io["L0_ffn_w1_s"], io["L0_ffn_w3_s"])):
                sp.dma_start(w13s[:, j, :].rearrange("p (n f) -> p n f", n=NS),
                             w.rearrange("n d f -> d n f")).then_inc(q["l_ws"], 16)
            sp.dma_start(w2s[:], io["L0_ffn_w2_s"].rearrange("n f d -> (n f) d")
                         .rearrange("(c p) d -> p c d", p=P)).then_inc(q["l_ws"], 16)
            for b in range(B):
                if b > 0:
                    for s in range(2):
                        sp.wait_ge(q["f_dn"], NG * (E - 2 + s) + NG + 2)
                        load_expert(s, s)
                with sp.Fori(1, E // 2) as e2:
                    for s in range(2):
                        sp.wait_ge(q["f_dn"], e2 * (2 * NG) + (NG * (s - 1) + 2 + NG * (E + 1) * b))
                        load_expert(e2 * 2 + s, s)
            for b in range(B):
                sp.wait_ge(q["o_add"], b + 1)
                sp.dma_start(out_v[:, NT * b:NT * b + NT, :], x1[:, NT * b:NT * b + NT, :]).then_inc(q["out_done"], 16)
            sp.wait_ge(q["out_done"], 16 * B)

        @block.gpsimd
        def _(pool):
            pool.sem_inc(q["b_qs"], 2)
            pool.sem_inc(q["t_cs"], 1)
            pool.sem_inc(q["h_cp"], 2)
            pool.memset(ones[:], 1.0).then_inc(q["cst"], 1)
            pool.wait_ge(q["cst"], 1)
            pool.affine_select(out=ident[:], in_=ones[:], pattern=[[-1, P]], compare_op=ALU.is_equal, fill=0.0,
                               base=0, channel_multiplier=1).then_inc(q["cst"], 1)
            pool.affine_select(out=earlier[:], in_=ones[:, 0:E * E].rearrange("p (e j) -> p e j", e=E),
                               pattern=[[1, E], [-1, E]], compare_op=ALU.is_gt, fill=0.0,
                               base=0, channel_multiplier=0).then_inc(q["cst"], 1)
            pool.memset(v[:], 1.0).then_inc(q["zeroed"], 1)
            pool.memset(wcomb[:], 0.0).then_inc(q["zeroed"], 1)
            pool.memset(acc[:], 0.0).then_inc(q["acc0"], 1)

            pool.wait_ge(q["l_x"], 16 * B)
            pool.wait_ge(q["weights"], 1)
            for b in range(B):
                pool.tensor_tensor(x1[:, NT * b:NT * b + NT, :], x_sb[:, NT * b:NT * b + NT, :],
                                   biasg[:, b, :].unsqueeze(1).to_broadcast([P, NT, P]), ALU.add).then_inc(q["x1_0"], 1)

            def query_slots(i):
                for b in range(B):
                    pool.wait_ge(q["b_sc"], i * 2 + (b + 1))
                    pool.tensor_copy(qs[:, b, :], qk[:, i + NT * b, 0, :]).then_inc(q["b_qs"], 1)

            def combined_slot(m):
                pool.wait_ge(q["t_ct"], m)
                pool.tensor_copy(cs[:, 0:HD + MEM], om[:, m - 1, :]).then_inc(q["t_cs"], 1)

            pool.wait_ge(q["a_qk"], TT + 2)
            query_slots(0)
            pool.wait_ge(q["mem_d"], 1)
            with pool.Fori(1, NT) as i:
                query_slots(i)
                pool.wait_ge(q["b_no"], i * 2 + 1)
                combined_slot(i)
            pool.wait_ge(q["b_no"], TT + 1)
            combined_slot(NT)

            def second_norm(b):
                with pool.Fori(0, NT // 2) as i2:
                    for s in range(2):
                        n = i2 * 2 + (NT * b + s + 1)
                        pool.wait_ge(q["h_hs"], n + 2)
                        pool.tensor_copy(h2T[:, bass.ds((i2 * 2 + s) * P, P)], hs[:, s, :]).then_inc(q["h_cp"], 1)

            second_norm(0)
            with pool.Fori(NT + 1, TT + 1) as m:
                combined_slot(m)
            pool.wait_ge(q["o_add"], 1)
            pool.memset(acc[:], 0.0).then_inc(q["acc0"], 1)
            second_norm(1)

        @block.scalar
        def _(act):
            for dst, src in small[1:-2:2]:
                act.dma_start(dst, src).then_inc(q["l_small"], 16)
            for name in ("a_hs", "a_qk", "a_gl", "b_el", "h_hs", "f_sg"):
                act.sem_inc(q[name], 2)
            for name in ("t_e", "t_cc", "pt_ev"):
                act.sem_inc(q[name], 1)

            act.wait_ge(q["l_small"], ALL_SMALL)
            act.activation(sig[:, 0, :], cT[:], ACT.Exp, scale=-1.0).then_inc(q["c_exp"], 1)
            act.wait_ge(q["tr_w"], 1)
            for j, (src, rows) in enumerate(turns):
                n = src.shape[0]
                act.copy(turned[0:rows, j, 0:n], bank_of(4 + j // 4)[0:rows, (j % 4) * P:(j % 4) * P + n]).then_inc(q["tr_c"], 1)
            act.wait_ge(q["ln_st"], 1)
            act.activation(sdev[:], var[:], ACT.Sqrt).then_inc(q["ln_sd"], 1)

            act.wait_ge(q["modded"], 1)
            act.wait_ge(q["weights"], 1)
            with act.Fori(0, NT) as i:
                for b in range(B):
                    n = i * 2 + (b + 1)
                    act.wait_ge(q["a_tr"], n + 2)
                    act.wait_ge(q["a_pb"], n)
                    act.activation(hs[:, b, :], bank_of(b)[:, 0:P], ACT.Identity, scale=mcol[:, 1, b:b + 1],
                                   bias=mcol[:, 0, b:b + 1]).then_inc(q["a_hs"], 1)
                for b in range(B):
                    n = i * 2 + (b + 1)
                    act.wait_ge(q["a_pa"], n + 2)
                    act.copy(qk[:, i + NT * b, :, :],
                             bank_of(2 + b)[0:2 * HD, 0:2 * P].rearrange("p (a c) -> p a c", a=2)).then_inc(q["a_qk"], 1)
                    act.activation(gelu[:, b, :], bank_of(2 + b)[0:2 * HD, 2 * P:3 * P], ACT.Gelu,
                                   bias=bp[:, 0:1]).then_inc(q["a_gl"], 1)

            act.wait_ge(q["mem_s"], 1)
            act.activation(om[:, :, HD:HD + MEM], om[:, :, HD:HD + MEM], ACT.Exp).then_inc(q["mem_e"], 1)

            def turned_probs(k, slot, free, n):
                act.wait_ge(q["pt_tr"], k + 3)
                act.wait_ge(q[free], n)
                act.copy(et[:, slot, :, :].rearrange("p (a c) q -> p a (c q)", a=2), pb[2][:, :, :]).then_inc(q["pt_ev"], 1)

            def local_exp(i, b):
                n = i * 2 + (b + 1)
                act.wait_ge(q["b_nm"], n + 2)
                act.wait_ge(q["pt_tr"], i * 3 + (b + 1))
                act.activation(el[:, b, :].rearrange("p (a c) -> p a c", a=2), pb[0][:, :, :], ACT.Exp, scale=SCALE,
                               bias=nml[:, b:b + 1]).then_inc(q["b_el"], 1)

            def sparse_exp(m, tr):
                act.wait_ge(q["b_sn"], m * 2 if tr is None else TT)
                act.wait_ge(q["pt_tr"], m * 3 if tr is None else tr)
                act.activation(es[:], s_all[:, m - 1, :], ACT.Exp, bias=col(snmax, m - 1)).then_inc(q["t_e"], 1)

            def combined_copy(m):
                act.wait_ge(q["t_ct"], m + 1)
                act.wait_ge(q["t_xm"], m)
                act.copy(csT[:], bank_of(7)[:, P:2 * P]).then_inc(q["t_cc"], 1)

            def sparse_tail(m):
                sparse_exp(m, None)
                turned_probs(m * 3, 2, "t_pv", m)

            def local(i):
                for b in range(B):
                    local_exp(i, b)
                for b in range(B):
                    turned_probs(i * 3 + (b + 1), b, "b_pv", i * 2 + (b + 1))

            local(0)
            with act.Fori(1, NT) as i:
                sparse_tail(i)
                local(i)
                combined_copy(i)
            sparse_tail(NT)
            combined_copy(NT)

            def second_norm(b):
                act.wait_ge(q["h_st"], b + 1)
                act.activation(sdev[:, 0:NT], var[:, 0:NT], ACT.Sqrt).then_inc(q["h_sd"], 1)
                with act.Fori(0, NT // 2) as i2:
                    for s in range(2):
                        n = i2 * 2 + (NT * b + s + 1)
                        act.wait_ge(q["h_tr"], n + 2)
                        act.wait_ge(q["h_cp"], n)
                        act.wait_ge(q["h_lg"], n)
                        act.activation(hs[:, s, :], bank_of(s)[:, 0:P], ACT.Identity, scale=mcol[:, 3, b:b + 1],
                                       bias=mcol[:, 2, b:b + 1]).then_inc(q["h_hs"], 1)
                act.wait_ge(q["g_sub"], b + 1)
                act.activation(gates[:], lg[:], ACT.Exp).then_inc(q["g_exp"], 1)

            def expert(n0):
                for g in range(NG):
                    for c in range(FC):
                        n = n0 + (FC * g + c + 1)
                        act.wait_ge(q["f_up"], n + 2)
                        act.wait_ge(q["f_gu"], n)
                        act.activation(silu[:, c % 2, :], bank_of(c % 2), ACT.Silu).then_inc(q["f_sg"], 1)

            def experts(b):
                with act.Fori(0, E) as e:
                    expert(e * (NG * FC) + NG * FC * (E + 1) * b)
                expert(NG * FC * ((E + 1) * b + E))

            second_norm(0)
            experts(0)
            with act.Fori(NT + 1, TT + 1) as m:
                sparse_exp(m, m + (2 * NT + 2))
                turned_probs(m + 2 * NT, 2, "t_pv", m)
                combined_copy(m)
            second_norm(1)
            experts(1)

        @block.vector
        def _(dve):
            for name, n in (("a_xh", 2), ("a_ev", 6), ("b_nm", 2), ("b_se", 1), ("b_no", 1), ("t_p", 1), ("t_no", 1),
                            ("t_x1", 1), ("h_xh", 2), ("f_gu", 2), ("f_ac", 8)):
                dve.sem_inc(q[name], n)
            steps = [0]

            def step(ins):
                steps[0] += 1
                ins.then_inc(q["dve_step"], 1)
                dve.wait_ge(q["dve_step"], steps[0])

            dve.wait_ge(q["c_exp"], 1)
            dve.wait_ge(q["cst"], 3)
            step(dve.tensor_scalar(sig[:, 1, :], sig[:, 0, :], 1.0, None, ALU.add))
            step(dve.reciprocal(sig[:, 0, :], sig[:, 1, :]))
            step(dve.tensor_tensor(siluc[:], cT[:], sig[:, 0, :], ALU.mult))
            for b in range(B):
                step(dve.tensor_scalar(silub[:, b, :], ones[:], siluc[:, b:b + 1], None, ALU.mult))
            for j in range(2):
                step(dve.tensor_scalar(bwide[:, j, :], ones[0:HD, :], bcols[:, j:j + 1], None, ALU.mult))
            dve.tensor_copy(junk[0:1, 0:1], ones[0:1, 0:1]).then_inc(q["c_silu"], 1)

            def aggregate(t0, n, eps):
                st = stats[:, t0:t0 + n, :]
                step(dve.tensor_tensor(mean[:, 0:n], st[:, :, 1], st[:, :, 4], ALU.add))
                step(dve.tensor_tensor(lt[:, 0, 0:n], st[:, :, 1], st[:, :, 4], ALU.subtract))
                step(dve.tensor_tensor(lt[:, 1, 0:n], st[:, :, 2], st[:, :, 5], ALU.add))
                step(dve.tensor_tensor(lt[:, 0, 0:n], lt[:, 0, 0:n], lt[:, 0, 0:n], ALU.mult))
                step(dve.scalar_tensor_tensor(lt[:, 1, 0:n], lt[:, 0, 0:n], P / 4.0, lt[:, 1, 0:n], ALU.mult, ALU.add))
                step(dve.tensor_scalar(mean[:, 0:n], mean[:, 0:n], 0.5, None, ALU.mult))
                return dve.tensor_scalar(var[:, 0:n], lt[:, 1, 0:n], 1.0 / P, eps, ALU.mult, ALU.add)

            dve.wait_ge(q["l_x"], 16 * B)
            for t in range(TT):
                last = dve.bn_stats(stats[:, t, :], x_sb[:, t, :])
            step(last)
            aggregate(0, TT, 1e-5).then_inc(q["ln_st"], 1)

            dve.wait_ge(q["m_ps"], 1)
            mps = bank_of(6)[:, 0:4 * B].rearrange("p (k b) -> p k b", k=4)
            for k in range(4):
                step(dve.tensor_scalar(mcol[:, k, :], mps[:, k, :], float(k % 2), None, ALU.add))
            gps = bank_of(7).rearrange("p (k b d) -> p k b d", k=2, b=B)
            step(dve.tensor_copy(gate_rows[:], gps))
            step(dve.scalar_tensor_tensor(gabs, gate_rows[:], -1.0, gate_rows[:], ALU.mult, ALU.max))
            step(dve.tensor_scalar(gabs, gabs, 0.25, None, ALU.max))
            step(dve.tensor_scalar(gtmp, gate_rows[:], 0.0, 2.0, ALU.is_ge, ALU.mult))
            step(dve.scalar_tensor_tensor(gate_rows[:], gtmp, -1.0, gabs, ALU.add, ALU.mult))
            dve.tensor_copy(junk[0:1, 0:1], ones[0:1, 0:1]).then_inc(q["modded"], 1)

            dve.wait_ge(q["fold_ps"], 1)
            step(dve.tensor_copy(ab[:], bank_of(0)[0:HD, 0:2 * P].rearrange("p (a c) -> p a c", a=2)))
            dve.tensor_copy(junk[0:1, 0:1], ones[0:1, 0:1]).then_inc(q["fold_c"], 1)
            dve.wait_ge(q["fold_ps"], 2)
            dve.wait_ge(q["zeroed"], 2)
            f0, f1 = bank_of(1), bank_of(2)
            ga = gate_rows[:, 0, :, :]
            step(dve.tensor_copy(wrow[:, 2 * HD:2 * HD + MEM], f0[:, 0:MEM]))
            step(dve.tensor_copy(wp[:], f0[:, P:P + 2 * HD]))
            step(dve.tensor_tensor(bp[:], f0[0:2 * HD, 2 * P:2 * P + 1], pred1b[:], ALU.add))
            step(dve.tensor_tensor(wbias[:], wbias[:], f0[:, 3 * P:4 * P], ALU.add))
            for b in range(B):
                step(dve.tensor_tensor(wx[:, b, :], f1[:, 0:P], ga[:, b, :], ALU.mult))
                step(dve.tensor_tensor(wpr[:, b, :], f1[0:2 * HD, P:2 * P], ga[0:2 * HD, b, :], ALU.mult))
                step(dve.tensor_tensor(biasg[:, b, :], wbias[:], ga[:, b, :], ALU.mult))
                for r in (0, 3):
                    rows = slice(HD * r, HD * r + HD)
                    step(dve.tensor_tensor(wcomb[rows, b, :], wb[rows, :], ga[rows, b, :], ALU.mult))
                for r in range(2):
                    step(dve.tensor_tensor(wcomb[HD * (r + 1):HD * (r + 2), b, :], f1[HD * r:HD * (r + 1), 2 * P:3 * P],
                                           ga[HD * r:HD * (r + 1), b, :], ALU.mult))
            dve.wait_ge(q["tr_c"], len(turns))
            step(dve.tensor_copy(gateWT[:], turned[:, 5, 0:E]))

            dve.wait_ge(q["ln_sd"], 1)
            step(dve.reciprocal(rstd[:], sdev[:]))
            dve.tensor_copy(junk[0:1, 0:1], ones[0:1, 0:1]).then_inc(q["weights"], 1)

            dve.wait_ge(q["x1_0"], B)
            with dve.Fori(0, NT) as i:
                for b in range(B):
                    t = i + NT * b
                    dve.wait_ge(q["a_tr"], i * 2 + (b + 1))
                    dve.tensor_scalar(xh[:, b, :], x_sb[:, t, :], col(mean, t), col(rstd, t), ALU.subtract,
                                      ALU.mult).then_inc(q["a_xh"], 1)
                for b in range(B):
                    t = i + NT * b
                    dve.wait_ge(q["a_pb"], i * 2 + (b + 3))
                    ps = bank_of(4 + b)
                    dve.tensor_copy(v[:, t, :, 0:HD], ps[:, 0:2 * HD].rearrange("p (a c) -> p a c", a=2)).then_inc(q["a_ev"], 1)
                    dve.tensor_copy(om[:, t, HD:HD + MEM], ps[:, 2 * HD:2 * HD + MEM]).then_inc(q["a_ev"], 1)
                    dve.tensor_tensor(x1[:, t, :], x1[:, t, :], ps[:, P:2 * P], ALU.add).then_inc(q["a_ev"], 1)

            dve.wait_ge(q["a_ev"], 3 * TT + 6)
            mem = om[:, :, HD:HD + MEM]
            step(dve.tensor_reduce(mstat[:, 0, :], mem, X, ALU.max))
            dve.tensor_tensor(mem, mem, mstat[:, 0, :].unsqueeze(2).to_broadcast([P, TT, MEM]), ALU.subtract).then_inc(q["mem_s"], 1)
            dve.wait_ge(q["mem_e"], 1)
            step(dve.tensor_reduce(mstat[:, 1, :], mem, X, ALU.add))
            step(dve.reciprocal(mstat[:, 2, :], mstat[:, 1, :]))
            dve.tensor_tensor(mem, mem, mstat[:, 2, :].unsqueeze(2).to_broadcast([P, TT, MEM]), ALU.mult).then_inc(q["mem_d"], 1)

            def scores_in(i, b):
                n = i * 2 + (b + 1)
                t = i + NT * b
                dve.wait_ge(q["b_sl"], n)
                dve.wait_ge(q["b_el"], n)
                dve.tensor_scalar(junk[:].rearrange("p (a c) -> p a c", a=2), pb[0][:, :, :], -SCALE, None, ALU.mult,
                                  ALU.min, accum_out=nml[:, b:b + 1]).then_inc(q["b_nm"], 1)
                dve.wait_ge(q["b_sc"], n + 2)
                dve.tensor_scalar(s_all[:, t, :].rearrange("p (a c) -> p a c", a=2), pb[1][:, :, :], SCALE, None,
                                  ALU.mult, ALU.max, accum_out=col(smax, t)).then_inc(q["b_se"], 1)
                dve.wait_ge(q["b_se"], n + 1)
                dve.tensor_scalar(col(snmax, t), col(smax, t), -1.0, None, ALU.mult).then_inc(q["b_sn"], 1)

            def local_out(i, b):
                n = i * 2 + (b + 1)
                dve.wait_ge(q["b_pv"], n + 2)
                dve.reciprocal(rl[:, b:b + 1], bank_of(6)[:, HD:HD + 1]).then_inc(q["b_rl"], 1)
                dve.wait_ge(q["b_rl"], n)
                dve.tensor_scalar(om[:, i + NT * b, 0:HD], bank_of(6)[:, 0:HD], rl[:, b:b + 1], None,
                                  ALU.mult).then_inc(q["b_no"], 1)

            KSTEPS = 2 * ROUNDS

            def largest(t, lo, hi):
                k0 = t * KSTEPS
                for r in range(lo, hi):
                    if r == 0:
                        dve.tensor_copy(kwork[:], s_all[:, t, :]).then_inc(q["k_ch"], 1)
                    dve.wait_ge(q["k_ch"], k0 + (2 * r + 1))
                    dve.memset(tick[:], 0.0)
                    dve.max(k8[:], kwork[:]).then_inc(q["k_ch"], 1)
                    dve.wait_ge(q["k_ch"], k0 + (2 * r + 2))
                    if r < ROUNDS - 1:
                        dve.memset(tick[:], 0.0)
                        dve.match_replace(kwork[:], k8[:], kwork[:], NEG).then_inc(q["k_ch"], 1)
                    else:
                        dve.tensor_copy(col(thr, t), k8[:, (KTOP - 1) % 8:(KTOP - 1) % 8 + 1]).then_inc(q["thr_r"], 1)

            def sparse_mask(m):
                dve.wait_ge(q["t_e"], m + 1)
                dve.wait_ge(q["thr_r"], m)
                dve.scalar_tensor_tensor(es[:], s_all[:, m - 1, :], col(thr, m - 1), es[:], ALU.is_ge,
                                         ALU.mult).then_inc(q["t_p"], 1)

            def sparse_out(m):
                dve.wait_ge(q["t_pv"], m + 1)
                dve.reciprocal(rs[:], bank_of(7)[:, HD:HD + 1]).then_inc(q["t_rs"], 1)
                dve.wait_ge(q["t_rs"], m)
                dve.wait_ge(q["t_ct"], m)
                dve.tensor_scalar(cs[:, HD + MEM:P], bank_of(7)[:, 0:HD], rs[:, 0:1], None, ALU.mult).then_inc(q["t_no"], 1)

            def residual(m):
                dve.wait_ge(q["t_xm"], m + 1)
                dve.tensor_tensor(x1[:, m - 1, :], x1[:, m - 1, :], bank_of(7)[:, 2 * P:3 * P], ALU.add).then_inc(q["t_x1"], 1)
                dve.wait_ge(q["t_x1"], m + 1)
                dve.bn_stats(stats[:, m - 1, :], x1[:, m - 1, :]).then_inc(q["t_st"], 1)

            for b in range(B):
                scores_in(0, b)
            for b in range(B):
                local_out(0, b)
            largest(0, 0, ROUNDS)
            with dve.Fori(1, NT) as i:
                sparse_mask(i)
                scores_in(i, 0)
                sparse_out(i)
                scores_in(i, 1)
                largest(i, 0, 4)
                local_out(i, 0)
                largest(i, 4, 8)
                local_out(i, 1)
                largest(i, 8, ROUNDS)
                residual(i)
            sparse_mask(NT)
            sparse_out(NT)
            residual(NT)

            def second_norm(b):
                dve.wait_ge(q["t_st"], NT * (b + 1))
                aggregate(NT * b, NT, 1e-5).then_inc(q["h_st"], 1)
                dve.wait_ge(q["h_sd"], b + 1)
                dve.reciprocal(rstd[:, 0:NT], sdev[:, 0:NT]).then_inc(q["h_rs"], 1)
                dve.wait_ge(q["h_rs"], b + 1)
                with dve.Fori(0, NT // 2) as i2:
                    for s in range(2):
                        t = i2 * 2 + s
                        dve.wait_ge(q["h_tr"], i2 * 2 + (NT * b + s + 1))
                        dve.tensor_scalar(xh[:, s, :], x1[:, t + NT * b, :], col(mean, t), col(rstd, t), ALU.subtract,
                                          ALU.mult).then_inc(q["h_xh"], 1)
                dve.wait_ge(q["h_lg"], NT * (b + 1) + 2)
                lps = bank_of(2)[:, 0:NT * E].rearrange("p (t e) -> p t e", e=E)
                step(dve.tensor_reduce(g1[:], lps, X, ALU.max))
                dve.tensor_tensor(lg[:], lps, g1[:].unsqueeze(2).to_broadcast([P, NT, E]), ALU.subtract).then_inc(q["g_sub"], 1)
                dve.wait_ge(q["g_exp"], b + 1)
                step(dve.tensor_reduce(g1[:], gates[:], X, ALU.add))
                step(dve.reciprocal(g1[:], g1[:]))
                step(dve.tensor_tensor(gates[:], gates[:], g1[:].unsqueeze(2).to_broadcast([P, NT, E]), ALU.mult))
                mine = gates[:].unsqueeze(3).to_broadcast([P, NT, E, E])
                other = gates[:].unsqueeze(2).to_broadcast([P, NT, E, E])
                step(dve.tensor_tensor(cmp1, other, mine, ALU.is_gt))
                step(dve.tensor_tensor(cmp2, other, mine, ALU.is_equal))
                for t in range(NT):
                    last = dve.tensor_tensor(cmp2[:, t, :, :], cmp2[:, t, :, :], earlier[:], ALU.mult)
                step(last)
                step(dve.tensor_tensor(cmp1, cmp1, cmp2, ALU.add))
                step(dve.tensor_reduce(rank[:], cmp1, X, ALU.add))
                step(dve.tensor_scalar(rank[:], rank[:], 2.0, 0.5, ALU.is_lt, ALU.mult))
                step(dve.tensor_tensor(gates[:], gates[:], rank[:], ALU.mult))

            def chunks(n0, g, between=None):
                for c in range(FC):
                    n = n0 + (FC * g + c + 1)
                    dve.wait_ge(q["f_sg"], n + 2)
                    dve.tensor_tensor(gu[g][:, c, :], silu[:, c % 2, :], bank_of(2 + c % 2), ALU.mult).then_inc(q["f_gu"], 1)

            def weigh(ex, g, gate):
                dve.wait_ge(q["f_dn"], ex * NG + (g + 3))
                dve.wait_ge(q["f_ac"], ex * (NG * TG) + TG * (g + 1))
                for j in range(TG):
                    t = TG * g + j
                    dve.scalar_tensor_tensor(acc[:, t, :], bank_of(4 + g)[:, j * P:(j + 1) * P], gate(t), acc[:, t, :],
                                             ALU.mult, ALU.add).then_inc(q["f_ac"], 1)

            def experts(b, search):
                dve.wait_ge(q["acc0"], b + 1)
                with dve.Fori(0, E) as e:
                    ex = e + (E + 1) * b
                    parts = [0, 4, 7, 10, ROUNDS]
                    for g in range(NG):
                        chunks(ex * (NG * FC), g)
                        if search:
                            largest(e + NT, parts[g], parts[g + 1])
                    for g in range(NG):
                        weigh(ex, g, lambda t: gates[:, t, bass.ds(e, 1)])
                        if search:
                            largest(e + NT, parts[NG + g], parts[NG + g + 1])
                ex = (E + 1) * b + E
                for g in range(NG):
                    chunks(ex * (NG * FC), g)
                for g in range(NG):
                    weigh(ex, g, lambda t: 0.5 / NS)
                dve.wait_ge(q["f_ac"], (ex + 1) * (NG * TG) + 8)
                step(dve.tensor_tensor(acc[:], acc[:], gate_rows[:, 1, b, :].unsqueeze(1).to_broadcast([P, NT, P]), ALU.mult))
                own = x1[:, NT * b:NT * b + NT, :]
                dve.tensor_tensor(own, own, acc[:], ALU.add).then_inc(q["o_add"], 1)

            second_norm(0)
            experts(0, True)
            with dve.Fori(NT + 1, TT + 1) as m:
                sparse_mask(m)
                sparse_out(m)
                residual(m)
            second_norm(1)
            experts(1, False)

        @block.tensor
        def _(pe):
            for name in ("a_tr", "a_pa", "a_pb", "b_sc", "b_pv", "h_tr", "h_lg", "f_up", "f_dn"):
                pe.sem_inc(q[name], 2)
            for name in ("t_pv", "t_ct", "t_xm"):
                pe.sem_inc(q[name], 1)
            pe.sem_inc(q["pt_tr"], 3)

            def product(out, lhsT, rhs, start=True, stop=True):
                return pe.matmul(out, lhsT, rhs, start=start, stop=stop)

            pe.wait_ge(q["cst"], 3)
            pe.wait_ge(q["l_small"], ALL_SMALL)
            for j, (src, rows) in enumerate(turns):
                n = src.shape[0]
                last = pe.transpose(bank_of(4 + j // 4)[0:rows, (j % 4) * P:(j % 4) * P + n], src, ident[0:n, 0:n])
            last.then_inc(q["tr_w"], 1)

            pe.wait_ge(q["c_silu"], 1)
            pe.wait_ge(q["l_wmod"], 16)
            for j, k in enumerate((0, 1, 3, 4)):
                product(bank_of(6)[:, B * j:B * j + B], wmod[:, k * P:(k + 1) * P], siluc[:])
            for j, k in enumerate((2, 5)):
                for b in range(B):
                    last = product(bank_of(7)[:, (B * j + b) * P:(B * j + b + 1) * P], silub[:, b, :], wmod[:, k * P:(k + 1) * P])
            last.then_inc(q["m_ps"], 1)

            pe.wait_ge(q["tr_c"], len(turns))
            projT, predinT, bankT, memoutT, pred2T = (turned[0:HD, j, :] for j in range(5))
            for r in range(2):
                last = product(bank_of(0)[0:HD, r * P:(r + 1) * P], memoutT[:, HD * r:HD * (r + 1)], wb_mem[:])
            last.then_inc(q["fold_ps"], 1)
            f0, f1 = bank_of(1), bank_of(2)
            product(f0[:, 0:MEM], projT, bankT[:, 0:MEM])
            product(f0[:, P:P + 2 * HD], predinT, pred1[:])
            product(f0[0:2 * HD, 2 * P:2 * P + 1], pred1[:], bcols[:, 2:3])
            product(f0[:, 3 * P:4 * P], bwide[:, 0, :], wb_mem[:], True, False)
            product(f0[:, 3 * P:4 * P], bwide[:, 1, :], wb_pred[:], False, True)
            product(f1[0:2 * HD, P:2 * P], pred2T[:, 0:2 * HD], wb_pred[:])
            pe.wait_ge(q["fold_c"], 1)
            product(f1[:, 0:P], projT, ab[:, 0, :])
            product(f1[0:MEM, 2 * P:3 * P], bankT[:, 0:MEM], ab[:, 1, :]).then_inc(q["fold_ps"], 1)

            pe.wait_ge(q["weights"], 1)
            with pe.Fori(0, NT) as i:
                for b in range(B):
                    n = i * 2 + (b + 1)
                    pe.wait_ge(q["a_xh"], n + 2)
                    pe.wait_ge(q["a_hs"], n)
                    pe.transpose(bank_of(b)[:, 0:P], xh[:, b, :], ident[:]).then_inc(q["a_tr"], 1)
                for b in range(B):
                    n = i * 2 + (b + 1)
                    pe.wait_ge(q["a_hs"], n + 2)
                    pe.wait_ge(q["a_gl"], n)
                    pe.wait_ge(q["a_qk"], n)
                    pe.wait_ge(q["a_ev"], n * 3)
                    ps = bank_of(2 + b)
                    product(ps[0:2 * HD, 0:P], wq[:], hs[:, b, :])
                    product(ps[0:2 * HD, P:2 * P], wk[:], hs[:, b, :])
                    product(ps[0:2 * HD, 2 * P:3 * P], wp[:], hs[:, b, :]).then_inc(q["a_pa"], 1)
                    product(bank_of(4 + b)[:, 0:P], hs[:, b, :], wrow[:])
                    product(bank_of(4 + b)[:, P:2 * P], hs[:, b, :], wx[:, b, :], True, False)
                for b in range(B):
                    pe.wait_ge(q["a_gl"], i * 2 + (b + 3))
                    product(bank_of(4 + b)[:, P:2 * P], gelu[:, b, :], wpr[:, b, :], False, True).then_inc(q["a_pb"], 1)

            pe.wait_ge(q["a_qk"], TT + 2)
            pe.wait_ge(q["a_gl"], TT + 2)
            pe.wait_ge(q["a_ev"], 3 * TT + 6)

            def scores(i, b):
                n = i * 2 + (b + 1)
                pe.wait_ge(q["b_qs"], n + 2)
                pe.wait_ge(q["b_el"], n + 1)
                for half in range(2):
                    keys = slice(NT * b + 4 * half, NT * b + 4 * half + 4)
                    last = product(pb[0][:, half, :], qs[0:HD, b, :], qk[0:HD, keys, 1, :])
                last.then_inc(q["b_sl"], 1)
                pe.wait_ge(q["b_se"], n)
                for half in range(2):
                    keys = slice(NT * b + 4 * half, NT * b + 4 * half + 4)
                    last = product(pb[1][:, half, :], qs[HD:2 * HD, b, :], qk[HD:2 * HD, keys, 1, :])
                last.then_inc(q["b_sc"], 1)

            def turn(k, probs):
                pe.wait_ge(q["pt_ev"], k)
                for c in range(NT):
                    last = pe.transpose(pb[2][:, c // 4, (c % 4) * P:(c % 4 + 1) * P], probs[:, c * P:(c + 1) * P], ident[:])
                last.then_inc(q["pt_tr"], 1)

            def weighted(out, slot, b, head, done):
                for c in range(NT):
                    last = product(out[:, 0:HD + 1], et[:, slot, c, :], v[:, NT * b + c, head, :], c == 0, c == NT - 1)
                last.then_inc(q[done], 1)

            def local(i, b):
                n = i * 2 + (b + 1)
                pe.wait_ge(q["b_el"], n + 2)
                turn(i * 3 + (b + 1), el[:, b, :])
                pe.wait_ge(q["pt_ev"], i * 3 + (b + 2))
                pe.wait_ge(q["b_no"], n)
                weighted(bank_of(6), b, b, 0, "b_pv")

            def sparse_turn(m, k):
                pe.wait_ge(q["t_p"], m + 1)
                turn(k, es[:, :])

            def sparse_product(m, k, b):
                pe.wait_ge(q["pt_ev"], k + 1)
                pe.wait_ge(q["t_x1"], m)
                weighted(bank_of(7), 2, b, 1, "t_pv")

            def combine(m, b):
                pe.wait_ge(q["t_cs"], m + 1)
                pe.wait_ge(q["t_no"], m + 1)
                pe.transpose(bank_of(7)[:, P:2 * P], cs[:], ident[:]).then_inc(q["t_ct"], 1)
                pe.wait_ge(q["t_cc"], m + 1)
                product(bank_of(7)[:, 2 * P:3 * P], csT[:], wcomb[:, b, :]).then_inc(q["t_xm"], 1)

            for b in range(B):
                scores(0, b)
            for b in range(B):
                local(0, b)
            with pe.Fori(1, NT) as i:
                sparse_turn(i, i * 3)
                scores(i, 0)
                sparse_product(i, i * 3, 0)
                scores(i, 1)
                local(i, 0)
                local(i, 1)
                combine(i, 0)
            sparse_turn(NT, NT * 3)
            sparse_product(NT, NT * 3, 0)
            combine(NT, 0)

            def second_norm(b):
                with pe.Fori(0, NT // 2) as i2:
                    for s in range(2):
                        n = i2 * 2 + (NT * b + s + 1)
                        pe.wait_ge(q["h_xh"], n + 2)
                        pe.wait_ge(q["h_hs"], n)
                        pe.transpose(bank_of(s)[:, 0:P], xh[:, s, :], ident[:]).then_inc(q["h_tr"], 1)
                        pe.wait_ge(q["h_hs"], n + 2)
                        product(bank_of(2)[:, bass.ds((i2 * 2 + s) * E, E)], hs[:, s, :], gateWT[:]).then_inc(q["h_lg"], 1)
                pe.wait_ge(q["h_cp"], NT * (b + 1) + 2)
                pe.wait_ge(q["g_sub"], b + 1)

            def expert(ex, up, down):
                for g in range(NG):
                    for c in range(FC):
                        pe.wait_ge(q["f_gu"], ex * (NG * FC) + (FC * g + c + 1))
                        for j in range(2):
                            last = product(bank_of(2 * j + c % 2), up(j)[:, c * P:(c + 1) * P], h2T[:, g * GRP:(g + 1) * GRP])
                        last.then_inc(q["f_up"], 1)
                for g in range(NG):
                    pe.wait_ge(q["f_gu"], ex * (NG * FC) + (FC * (g + 1) + 2))
                    pe.wait_ge(q["f_ac"], ex * (NG * TG) + TG * (g + 1))
                    for j in range(TG):
                        for c in range(FC):
                            last = product(bank_of(4 + g)[:, j * P:(j + 1) * P], gu[g][:, c, j * P:(j + 1) * P], down[:, c, :],
                                           c == 0, c == FC - 1)
                    last.then_inc(q["f_dn"], 1)

            def experts(b):
                with pe.Fori(0, E // 2) as e2:
                    for s in range(2):
                        pe.wait_ge(l_w[s], e2 * 48 + 48 * (E // 2 * b + 1))
                        expert(e2 * 2 + (s + (E + 1) * b), lambda j: w13[:, s, j, :], w2[:, s, :, :])
                pe.wait_ge(q["l_ws"], 48)
                expert((E + 1) * b + E, lambda j: w13s[:, j, :], w2s)

            second_norm(0)
            experts(0)
            pe.wait_ge(q["f_ac"], (E + 1) * NG * TG + 8)
            with pe.Fori(NT + 1, TT + 1) as m:
                sparse_turn(m, m + 2 * NT)
                sparse_product(m, m + 2 * NT, 1)
                combine(m, 1)
            second_norm(1)
            experts(1)


_INS = ['L0_attn_x', 'L0_attn_local_qkv_w', 'L0_attn_sparse_qkv_w', 'L0_attn_memory_bank', 'L0_attn_memory_proj_w',
        'L0_attn_mem_out_w', 'L0_attn_mem_out_b', 'L0_attn_pred_in_w', 'L0_attn_pred_in_b', 'L0_attn_pred1_w',
        'L0_attn_pred1_b', 'L0_attn_pred2_w', 'L0_attn_pred2_b', 'L0_attn_warboss_w', 'L0_attn_warboss_b',
        'L0_ffn_gate_W', 'L0_ffn_w1_e', 'L0_ffn_w3_e', 'L0_ffn_w2_e', 'L0_ffn_w1_s', 'L0_ffn_w3_s', 'L0_ffn_w2_s',
        'L0_c', 'L0_wmod']


def kernel(**inputs):
    import numpy as _np
    import concourse.bacc as _bacc
    from concourse import mybir as _mybir
    from concourse.bass_utils import run_bass_kernel_spmd as _run

    nc = _bacc.Bacc("TRN2", target_bir_lowering=False, num_devices=1)
    arrays, io = {}, {}
    for name in _INS:
        a = _np.ascontiguousarray(inputs[name])
        arrays[f"in_{name}_dram"] = a
        io[name] = nc.dram_tensor(f"in_{name}_dram", a.shape, _mybir.dt.from_np(a.dtype), kind="ExternalInput").ap()
    io["out"] = nc.dram_tensor("out_0_dram", inputs["L0_attn_x"].shape, _mybir.dt.float32, kind="ExternalOutput").ap()
    build(nc, io)
    r = _run(nc, [arrays], core_ids=[0])
    return r.results[0]["out_0_dram"]
```

```python
import math
from contextlib import ExitStack

import concourse.bass as bass
from concourse import mybir

F32 = mybir.dt.float32
BF16 = mybir.dt.bfloat16
ALU = mybir.AluOpType
ACT = mybir.ActivationFunctionType
X = mybir.AxisListType.X

P = 128
NEG = -3.0e38


def normal_quantile(tail):
    low, high = 0.0, 8.0
    for _ in range(60):
        mid = (low + high) / 2
        low, high = (mid, high) if math.erfc(mid / math.sqrt(2)) / 2 > tail else (low, mid)
    return low


def build(nc, io):
    x_d, out_d = io["L0_attn_x"], io["out"]
    B, S, D = x_d.shape
    HD = io["L0_attn_memory_bank"].shape[1]
    MEM = io["L0_attn_memory_bank"].shape[0]
    E, _, F = io["L0_ffn_w1_e"].shape
    NS, _, FS = io["L0_ffn_w1_s"].shape
    NT = S // P
    TT = B * NT
    FC = F // P
    KTOP = max(1, int(S * 0.1))
    ROUNDS = (KTOP + 7) // 8
    SCALE = HD ** -0.5
    GRP = 512
    NG = S // GRP
    TG = GRP // P
    assert B == 2 and D == P and NS * FS == F and HD == 32 and MEM == 64 and E == NT

    ctx = ExitStack()
    with ctx:
        def sb(name, shape, dt=F32):
            return ctx.enter_context(nc.sbuf_tensor(name, shape, dt))

        def sem(name):
            return ctx.enter_context(nc.semaphore(name))

        ident = sb("ident", [P, P])
        ones = sb("ones", [P, P])
        earlier = sb("earlier", [P, E, E])
        cT = sb("cT", [P, B])
        sig = sb("sig", [P, 2, B])
        siluc = sb("siluc", [P, B])
        silub = sb("silub", [P, B, P])
        wmod = sb("wmod", [P, 6 * P])
        mcol = sb("mcol", [P, 4, B])
        gate_rows = sb("gate_rows", [P, 2, B, P])
        wqk = sb("wqk", [P, 2, 2 * HD])
        wrow = sb("wrow", [P, B, 2 * P])
        proj = sb("proj", [P, HD])
        predin = sb("predin", [P, HD])
        bank = sb("bank", [MEM, HD])
        memout = sb("memout", [2 * HD, HD])
        pred2 = sb("pred2", [2 * HD, HD])
        gateW = sb("gateW", [E, P])
        gateWT = sb("gateWT", [P, E])
        pred1 = sb("pred1", [HD, 2 * HD])
        pred1b = sb("pred1b", [2 * HD, 1])
        bcols = sb("bcols", [HD, 3])
        bwide = sb("bwide", [HD, 2, P])
        wb = sb("wb", [P, P])
        wb_mem = sb("wb_mem", [HD, P])
        wb_pred = sb("wb_pred", [HD, P])
        wbias = sb("wbias", [P, P])
        turned = sb("turned", [P, 6, P])
        ab = sb("ab", [HD, 2, P])
        wp = sb("wp", [P, 2 * HD])
        bp = sb("bp", [2 * HD, 1])
        wcomb = sb("wcomb", [P, B, P])
        wpr = sb("wpr", [2 * HD + 1, B, P])
        x_sb = sb("x_sb", [P, TT, P])
        x1 = sb("x1", [P, TT, P])
        stats = sb("stats", [P, TT, 6])
        mean = sb("mean", [P, TT])
        var = sb("var", [P, TT])
        sdev = sb("sdev", [P, TT])
        rstd = sb("rstd", [P, TT])
        lt = sb("lt", [P, 2, TT])
        xh = sb("xh", [P, 2, B, P])
        hs = sb("hs", [P, 2, B, P])
        qk = sb("qk", [2 * HD, TT, 2, P])
        gelu = sb("gelu", [2 * HD + 1, B, P])
        v = sb("v", [P, TT, 2, HD + 1])
        om = sb("om", [P, TT, HD + MEM])
        mstat = sb("mstat", [P, 3, TT])
        qs = sb("qs", [2 * HD, 2, P])
        s_all = sb("s_all", [P, TT, S])
        v_bt = v[:].rearrange("p (b t) h c -> p b t h c", b=B)
        om_bt = om[:].rearrange("p (b t) c -> p b t c", b=B)
        x1_bt = x1[:].rearrange("p (b t) d -> p b t d", b=B)
        x_bt = x_sb[:].rearrange("p (b t) d -> p b t d", b=B)
        qk_bt = qk[:].rearrange("p (b t) k d -> p b t k d", b=B)
        smax = sb("smax", [P, TT])
        snmax = sb("snmax", [P, TT])
        thr = sb("thr", [P, TT])
        junk = sb("junk", [P, S], BF16)
        nml = sb("nml", [P, 2])
        el = sb("el", [P, 2, S])
        et = sb("et", [P, 2, NT, P])
        rl = sb("rl", [P, 2])
        rs = sb("rs", [P, 2])
        kwork = sb("kwork", [P, S])
        k8 = sb("k8", [P, 8])
        k16 = sb("k16", [P, 16])
        krank = sb("krank", [P, 16])
        kpick = sb("kpick", [P, 16])
        ajunk = sb("ajunk", [P, S], BF16)
        kabs = sb("kabs", [P, 1])
        kstep = sb("kstep", [P, 1])
        ksum = sb("ksum", [P, 1])
        kmove = sb("kmove", [P, 1])
        kneg = sb("kneg", [P, 4 * TT])
        kguess = sb("kguess", [P, 1])
        kcount = sb("kcount", [P, 1])
        kfound = sb("kfound", [P, 1])
        kflag = sb("kflag", [1, 1], mybir.dt.int32)
        tick = sb("tick", [1, 1])
        gabs = kwork[:, 0:S // 2].rearrange("p (k b d) -> p k b d", k=2, b=B)
        cs = sb("cs", [P, 2, P])
        csT = sb("csT", [P, 2, P])
        h2T = sb("h2T", [P, S])
        lg = sb("lg", [P, NT, E])
        g1 = sb("g1", [P, NT])
        cmp1, cmp2 = (kwork[:, h * S // 2:(h + 1) * S // 2].rearrange("p (t e j) -> p t e j", t=NT, e=E) for h in range(2))
        rank = sb("rank", [P, NT, E])
        gates = sb("gates", [P, NT, E])
        w13 = sb("w13", [P, 2, 2, F])
        w2 = sb("w2", [P, 2, FC, P])
        w13s = sb("w13s", [P, 2, F])
        w2s = sb("w2s", [P, FC, P])
        silu = sb("silu", [P, 2, GRP])
        gu = [el[:, :, :].rearrange("p a (c t) -> p (a c) t", t=GRP),
              sb("gu1", [P, FC, GRP])]
        acc = sb("acc", [P, NT, P])

        pb = [ctx.enter_context(nc.psum_tensor(f"pb{n}", [P, 2, 512], F32)) for n in range(4)]

        def bank_of(n):
            return pb[n // 2][:, n % 2, :]

        names = """l_c l_x l_wmod l_small l_w0 l_w1 l_ws cst filled acc0 c_exp c_silu m_ps gb_raw gb_done
        tr_w tr_c fold_ps fold_c weights ln_st ln_sd
        a_xh a_tr a_hs a_pa a_qk a_gl a_pb a_ev mem_s mem_e mem_d
        b_qs b_sl b_sc b_nm b_se b_sn b_el b_tr b_ev b_pv b_rl b_no
        k_abs k_cnt k_up k_u k_th k_y k_m1 k_r k_m2 thr_r k_good k_sum k_flag k_slow0 k_slow1
        t_e t_p t_tr t_ev t_pv t_rs t_no t_cs t_ct t_cc t_xm t_x1 t_st
        h_st h_sd h_rs h_xh h_tr h_hs h_cp h_lg g_sub g_exp
        f_up f_sg f_gu f_dn f_ac o_add out_done dve_step""".split()
        q = {n: sem(n) for n in names}
        l_w = [q["l_w0"], q["l_w1"]]

        x_v = x_d.rearrange("b (t p) d -> p (b t) d", p=P)
        out_v = out_d.rearrange("b (t p) d -> p (b t) d", p=P)
        w1_d, w3_d, w2_d = io["L0_ffn_w1_e"], io["L0_ffn_w3_e"], io["L0_ffn_w2_e"]

        def column(a):
            return a.rearrange("(a b) -> a b", b=1)

        wlo, wsp, wbo = io["L0_attn_local_qkv_w"], io["L0_attn_sparse_qkv_w"], io["L0_attn_warboss_w"]
        small = [(proj[:], io["L0_attn_memory_proj_w"]), (predin[:], io["L0_attn_pred_in_w"]),
                 (bank[:], io["L0_attn_memory_bank"]), (memout[:], io["L0_attn_mem_out_w"]),
                 (pred2[:], io["L0_attn_pred2_w"]), (gateW[:], io["L0_ffn_gate_W"]),
                 (pred1[:], io["L0_attn_pred1_w"])]
        for k, w in enumerate((wlo, wsp)):
            small += [(wqk[:, 0, HD * k:HD * k + HD], w[:, 0:HD]), (wqk[:, 1, HD * k:HD * k + HD], w[:, HD:2 * HD])]
            small += [(wrow[:, b, HD * k:HD * k + HD], w[:, 2 * HD:3 * HD]) for b in range(B)]
        small += [(wb[0:HD, :], wbo[0:HD, :]), (wb[3 * HD:4 * HD, :], wbo[HD:2 * HD, :]),
                  (wb_mem[:], wbo[2 * HD:3 * HD, :]), (wb_pred[:], wbo[3 * HD:4 * HD, :]),
                  (wbias[:], io["L0_attn_warboss_b"].partition_broadcast(P)),
                  (pred1b[:], column(io["L0_attn_pred1_b"])), (bcols[:, 0:1], column(io["L0_attn_mem_out_b"])),
                  (bcols[:, 1:2], column(io["L0_attn_pred2_b"])), (bcols[:, 2:3], column(io["L0_attn_pred_in_b"]))]
        ALL_SMALL = 16 * len(small)

        def col(t, n):
            return t[:, n:n + 1] if isinstance(n, int) else t[:, bass.ds(n, 1)]

        turns = [(proj[:], HD), (predin[:], HD), (bank[:], HD), (memout[:], HD), (pred2[:], HD), (gateW[:], P)]

        block = ctx.enter_context(nc.Block())

        @block.sync
        def _(sp):
            for b in range(B):
                sp.dma_start(cT[:, b:b + 1], column(io["L0_c"][b])).then_inc(q["l_c"], 16)
            for b in range(B):
                sp.dma_start(x_sb[:, NT * b:NT * b + NT, :], x_v[:, NT * b:NT * b + NT, :]).then_inc(q["l_x"], 16)
            for dst, src in small[0::2]:
                sp.dma_start(dst, src).then_inc(q["l_small"], 16)

            def load_expert(e, s):
                for j, w in enumerate((w1_d, w3_d)):
                    sp.dma_start(w13[:, s, j, :], w[e]).then_inc(l_w[s], 16)
                sp.dma_start(w2[:, s, :, :], w2_d[e].rearrange("(c p) d -> p c d", p=P)).then_inc(l_w[s], 16)

            for s in range(2):
                load_expert(s, s)
            for j, w in enumerate((io["L0_ffn_w1_s"], io["L0_ffn_w3_s"])):
                sp.dma_start(w13s[:, j, :].rearrange("p (n f) -> p n f", n=NS),
                             w.rearrange("n d f -> d n f")).then_inc(q["l_ws"], 16)
            sp.dma_start(w2s[:], io["L0_ffn_w2_s"].rearrange("n f d -> (n f) d")
                         .rearrange("(c p) d -> p c d", p=P)).then_inc(q["l_ws"], 16)
            for b in range(B):
                for s in range(2):
                    if b > 0:
                        sp.wait_ge(q["f_dn"], NG * ((E + 1) * b - 2 + s + 1) + 2)
                        load_expert(s, s)
                with sp.Fori(1, E // 2) as e2:
                    for s in range(2):
                        sp.wait_ge(q["f_dn"], e2 * (2 * NG) + (NG * s + 2 + NG * (E + 1) * b))
                        load_expert(e2 * 2 + s, s)
            for b in range(B):
                sp.wait_ge(q["o_add"], b + 1)
                sp.dma_start(out_v[:, NT * b:NT * b + NT, :], x1[:, NT * b:NT * b + NT, :]).then_inc(q["out_done"], 16)
            sp.wait_ge(q["out_done"], 16 * B)

        @block.gpsimd
        def _(pool):
            for name in ("b_qs", "t_cs", "h_cp"):
                pool.sem_inc(q[name], 2)
            pool.memset(ones[:], 1.0).then_inc(q["cst"], 1)
            pool.wait_ge(q["cst"], 1)
            pool.affine_select(out=ident[:], in_=ones[:], pattern=[[-1, P]], compare_op=ALU.is_equal, fill=0.0,
                               base=0, channel_multiplier=1).then_inc(q["cst"], 1)
            pool.affine_select(out=earlier[:], in_=ones[:, 0:E * E].rearrange("p (e j) -> p e j", e=E),
                               pattern=[[1, E], [-1, E]], compare_op=ALU.is_gt, fill=0.0,
                               base=0, channel_multiplier=0).then_inc(q["cst"], 1)
            pool.iota(krank[:], pattern=[[-1, 16]], base=KTOP - 1, channel_multiplier=0,
                      allow_small_or_imprecise_dtypes=True).then_inc(q["cst"], 1)
            pool.memset(gelu[:], 1.0).then_inc(q["filled"], 1)
            pool.memset(v[:], 1.0).then_inc(q["filled"], 1)
            pool.memset(acc[:], 0.0).then_inc(q["acc0"], 1)

            pool.wait_ge(q["gb_raw"], 1)
            gb = gate_rows[:, 1, :, :]
            g_abs, g_sign = csT[:], cs[:]
            pool.tensor_scalar(g_sign, gb, 0.0, 2.0, ALU.is_ge, ALU.mult).then_inc(q["gb_done"], 1)
            pool.wait_ge(q["gb_done"], 1)
            pool.tensor_scalar(g_sign, g_sign, -1.0, None, ALU.add).then_inc(q["gb_done"], 1)
            pool.wait_ge(q["gb_done"], 2)
            pool.tensor_tensor(g_abs, g_sign, gb, ALU.mult).then_inc(q["gb_done"], 1)
            pool.wait_ge(q["gb_done"], 3)
            pool.tensor_scalar(g_abs, g_abs, 0.25, None, ALU.max).then_inc(q["gb_done"], 1)
            pool.wait_ge(q["gb_done"], 4)
            pool.tensor_tensor(gb, g_abs, g_sign, ALU.mult).then_inc(q["gb_done"], 1)

            pool.wait_ge(q["a_qk"], 2 * NT + 4)
            with pool.Fori(0, NT) as i:
                for b in range(B):
                    pool.wait_ge(q["b_sc"], i * 2 + (b + 1))
                    pool.tensor_copy(qs[:, b, :], qk[:, i + NT * b, 0, :]).then_inc(q["b_qs"], 1)

            def combined_slot(m, s):
                pool.wait_ge(q["t_ct"], m)
                pool.tensor_copy(cs[:, s, 0:HD + MEM], om[:, m - 1, :]).then_inc(q["t_cs"], 1)

            def sparse_tail(b):
                with pool.Fori(0, NT // 2) as i2:
                    for s in range(2):
                        combined_slot(i2 * 2 + (NT * b + s + 1), s)

            def second_norm(b):
                with pool.Fori(0, NT // 2) as i2:
                    for s in range(2):
                        n = i2 * 2 + (NT * b + s + 1)
                        pool.wait_ge(q["h_hs"], n + 2)
                        pool.tensor_copy(h2T[:, bass.ds((i2 * 2 + s) * P, P)], hs[:, s, 0, :]).then_inc(q["h_cp"], 1)

            pool.wait_ge(q["b_no"], TT + 2)
            pool.wait_ge(q["mem_d"], 1)
            sparse_tail(0)
            second_norm(0)
            sparse_tail(1)
            pool.wait_ge(q["o_add"], 1)
            pool.memset(acc[:], 0.0).then_inc(q["acc0"], 1)
            second_norm(1)

        @block.scalar
        def _(act):
            act.dma_start(wmod[:], io["L0_wmod"]).then_inc(q["l_wmod"], 16)
            for dst, src in small[1::2]:
                act.dma_start(dst, src).then_inc(q["l_small"], 16)
            for name in ("a_hs", "b_el", "b_ev", "t_e", "t_ev", "t_cc", "h_hs", "f_sg"):
                act.sem_inc(q[name], 1 if name == "b_ev" else 2)
            for name in ("a_qk", "a_gl"):
                act.sem_inc(q[name], {"a_qk": 4, "a_gl": 1}[name])

            act.wait_ge(q["l_c"], 16 * B)
            act.activation(sig[:, 0, :], cT[:], ACT.Exp, scale=-1.0).then_inc(q["c_exp"], 1)
            act.wait_ge(q["ln_st"], 1)
            act.activation(sdev[:], var[:], ACT.Sqrt).then_inc(q["ln_sd"], 1)
            act.preload_act_table(ACT.Gelu)
            act.wait_ge(q["tr_w"], 1)
            for j, (src, rows) in enumerate(turns):
                n = src.shape[0]
                act.copy(turned[0:rows, j, 0:n], bank_of(4 + j // 4)[0:rows, (j % 4) * P:(j % 4) * P + n]).then_inc(q["tr_c"], 1)

            def first_h(n, s):
                act.wait_ge(q["a_tr"], n + 2)
                act.wait_ge(q["a_pb"], n)
                for b in range(B):
                    last = act.activation(hs[:, s, b, :], bank_of(s)[:, b * P:(b + 1) * P], ACT.Identity,
                                          scale=mcol[:, 1, b:b + 1], bias=mcol[:, 0, b:b + 1])
                last.then_inc(q["a_hs"], 1)

            def pair_out(i, n, s):
                act.wait_ge(q["a_pa"], n + 2)
                act.wait_ge(q["a_pb"], n + 1)
                pair = bank_of(2 + s).rearrange("p (k b d) -> p k b d", k=2, b=B)
                act.activation(gelu[0:2 * HD, :, :], pair[0:2 * HD, 1, :, :], ACT.Gelu, bias=bp[:, 0:1]).then_inc(q["a_gl"], 1)
                for k in range(2):
                    act.copy(qk_bt[:, :, i, k, :], pair[2 * HD * k:2 * HD * (k + 1), 0, :, :]).then_inc(q["a_qk"], 1)

            act.wait_ge(q["weights"], 1)
            act.wait_ge(q["filled"], 1)
            first_h(1, 0)
            with act.Fori(0, NT // 2 - 1) as i2:
                for s in range(2):
                    i = i2 * 2 + s
                    first_h(i + 2, 1 - s)
                    pair_out(i, i + 1, s)
            first_h(NT, 1)
            for s in range(2):
                pair_out(NT - 2 + s, NT - 1 + s, s)

            act.preload_act_table(ACT.Exp)
            act.wait_ge(q["mem_s"], 1)
            act.activation(om[:, :, HD:HD + MEM], om[:, :, HD:HD + MEM], ACT.Exp).then_inc(q["mem_e"], 1)

            def local_exp(i, b):
                n = i * 2 + (b + 1)
                act.wait_ge(q["b_nm"], n + 2)
                act.wait_ge(q["b_tr"], n)
                act.activation(el[:, b, :].rearrange("p (a c) -> p a c", a=2), pb[0][:, :, :], ACT.Exp, scale=SCALE,
                               bias=nml[:, b:b + 1]).then_inc(q["b_el"], 1)

            def turned_local(i, b):
                n = i * 2 + (b + 1)
                act.wait_ge(q["b_tr"], n + 2)
                act.wait_ge(q["b_pv"], n)
                act.copy(et[:, b, :, :].rearrange("p (a c) q -> p a (c q)", a=2), pb[2][:, :, :]).then_inc(q["b_ev"], 1)

            def spread(t):
                act.wait_ge(q["k_up"], t * 4 + 1)
                act.activation(ajunk[:, 0:S // 2], s_all[:, t, 0:S // 2], ACT.Abs, accum_out=kabs[:]).then_inc(q["k_abs"], 1)

            def count(t, r):
                act.wait_ge(q["k_up"], t * 4 + (r + 2))
                act.activation(ajunk[:], s_all[:, t, :], ACT.Sign, bias=col(kneg, t * 4 + r), accum_out=ksum[:]).then_inc(q["k_cnt"], 1)

            def scores_and_search(i, t):
                if t is not None:
                    act.wait_ge(q["b_sn"], t * 2 + 1)
                    spread(t)
                local_exp(i, 0)
                if t is not None:
                    count(t, 0)
                turned_local(i, 0)
                if t is not None:
                    count(t, 1)
                local_exp(i, 1)
                if t is not None:
                    count(t, 2)
                turned_local(i, 1)

            scores_and_search(0, None)
            with act.Fori(1, NT) as i:
                scores_and_search(i, i - 1)
            act.wait_ge(q["b_sn"], TT)
            spread(NT - 1)
            for r in range(3):
                count(NT - 1, r)

            def sparse_exp(m, s):
                act.wait_ge(q["t_tr"], m)
                act.activation(el[:, s, :], s_all[:, m - 1, :], ACT.Exp, bias=col(snmax, m - 1)).then_inc(q["t_e"], 1)

            def turned_sparse(m, s):
                act.wait_ge(q["t_tr"], m + 2)
                act.wait_ge(q["t_pv"], m)
                act.copy(et[:, s, :, :].rearrange("p (a c) q -> p a (c q)", a=2), pb[2 - s][:, :, :]).then_inc(q["t_ev"], 1)

            def combined_copy(m, s):
                act.wait_ge(q["t_ct"], m + 2)
                act.wait_ge(q["t_xm"], m)
                act.copy(csT[:, s, :], bank_of(6 + s)[:, P:2 * P]).then_inc(q["t_cc"], 1)

            def stage(b, k, s, parts="etc"):
                m = k + (NT * b + 1)
                if "e" in parts:
                    sparse_exp(m + 1, 1 - s)
                if "t" in parts:
                    turned_sparse(m, s)
                if "c" in parts:
                    combined_copy(m - 2, s)

            def sparse_tail(b):
                stage(b, -1, 1, "e")
                stage(b, 0, 0, "et")
                stage(b, 1, 1, "et")
                with act.Fori(1, NT // 2 - 1) as i2:
                    for s in range(2):
                        stage(b, i2 * 2 + s, s)
                stage(b, NT - 2, 0)
                stage(b, NT - 1, 1, "tc")
                stage(b, NT, 0, "c")
                stage(b, NT + 1, 1, "c")

            def second_norm(b):
                act.wait_ge(q["h_st"], b + 1)
                act.activation(sdev[:, 0:NT], var[:, 0:NT], ACT.Sqrt).then_inc(q["h_sd"], 1)
                with act.Fori(0, NT // 2) as i2:
                    for s in range(2):
                        n = i2 * 2 + (NT * b + s + 1)
                        act.wait_ge(q["h_tr"], n + 2)
                        act.wait_ge(q["h_cp"], n)
                        act.wait_ge(q["h_lg"], n)
                        act.activation(hs[:, s, 0, :], bank_of(s)[:, 0:P], ACT.Identity, scale=mcol[:, 3, b:b + 1],
                                       bias=mcol[:, 2, b:b + 1]).then_inc(q["h_hs"], 1)
                act.wait_ge(q["g_sub"], b + 1)
                act.activation(gates[:], lg[:], ACT.Exp).then_inc(q["g_exp"], 1)
                act.preload_act_table(ACT.Silu)

            def expert(place, t=None):
                for k in range(NG * FC):
                    n = place * (NG * FC) + (k + 1)
                    act.wait_ge(q["f_up"], n + 2)
                    act.wait_ge(q["f_gu"], n)
                    act.activation(silu[:, k % 2, :], bank_of(k % 2), ACT.Silu).then_inc(q["f_sg"], 1)
                    if t is not None:
                        if k == 0:
                            spread(t)
                        if k in (2, 4, 6):
                            count(t, (k - 2) // 2)

            def experts(b):
                expert((E + 1) * b)
                with act.Fori(0, E) as e:
                    expert(e + ((E + 1) * b + 1), e + NT if b == 0 else None)

            for b in range(B):
                sparse_tail(b)
                second_norm(b)
                experts(b)
                if b == 0:
                    act.preload_act_table(ACT.Exp)
                    act.wait_ge(q["f_dn"], (E + 1) * NG + 2)

        @block.vector
        def _(dve):
            for name, n in (("a_xh", 2), ("a_ev", 6), ("b_nm", 2), ("b_se", 1), ("b_no", 2), ("t_p", 2), ("t_no", 2),
                            ("t_x1", 2), ("h_xh", 2), ("f_gu", 2), ("f_ac", 8), ("k_up", 1)):
                dve.sem_inc(q[name], n)
            steps = [0]

            def step(ins):
                steps[0] += 1
                ins.then_inc(q["dve_step"], 1)
                dve.wait_ge(q["dve_step"], steps[0])

            def aggregate(t0, n, eps):
                st = stats[:, t0:t0 + n, :]
                step(dve.tensor_tensor(mean[:, 0:n], st[:, :, 1], st[:, :, 4], ALU.add))
                step(dve.tensor_tensor(lt[:, 0, 0:n], st[:, :, 1], st[:, :, 4], ALU.subtract))
                step(dve.tensor_tensor(lt[:, 1, 0:n], st[:, :, 2], st[:, :, 5], ALU.add))
                step(dve.tensor_tensor(lt[:, 0, 0:n], lt[:, 0, 0:n], lt[:, 0, 0:n], ALU.mult))
                step(dve.scalar_tensor_tensor(lt[:, 1, 0:n], lt[:, 0, 0:n], P / 4.0, lt[:, 1, 0:n], ALU.mult, ALU.add))
                step(dve.tensor_scalar(mean[:, 0:n], mean[:, 0:n], 0.5, None, ALU.mult))
                return dve.tensor_scalar(var[:, 0:n], lt[:, 1, 0:n], 1.0 / P, eps, ALU.mult, ALU.add)

            dve.wait_ge(q["c_exp"], 1)
            dve.wait_ge(q["cst"], 4)
            step(dve.tensor_scalar(sig[:, 1, :], sig[:, 0, :], 1.0, None, ALU.add))
            step(dve.reciprocal(sig[:, 0, :], sig[:, 1, :]))
            step(dve.tensor_tensor(siluc[:], cT[:], sig[:, 0, :], ALU.mult))
            for b in range(B):
                last = dve.tensor_scalar(silub[:, b, :], ones[:], siluc[:, b:b + 1], None, ALU.mult)
            last.then_inc(q["c_silu"], 1)
            dve.wait_ge(q["l_x"], 16 * B)
            for t in range(TT):
                last = dve.bn_stats(stats[:, t, :], x_sb[:, t, :])
            step(last)
            aggregate(0, TT, 1e-5).then_inc(q["ln_st"], 1)
            dve.wait_ge(q["l_small"], ALL_SMALL)
            for j in range(2):
                last = dve.tensor_scalar(bwide[:, j, :], ones[0:HD, :], bcols[:, j:j + 1], None, ALU.mult)
            last.then_inc(q["c_silu"], 1)

            dve.wait_ge(q["m_ps"], 1)
            mps = bank_of(6)[:, 0:4 * B].rearrange("p (k b) -> p k b", k=4)
            for k in range(4):
                dve.tensor_scalar(mcol[:, k, :], mps[:, k, :], float(k % 2), None, ALU.add)
            gps = bank_of(7).rearrange("p (k b d) -> p k b d", k=2, b=B)
            step(dve.tensor_copy(gate_rows[:], gps))
            dve.tensor_copy(tick[:], ones[0:1, 0:1]).then_inc(q["gb_raw"], 1)
            ga = gate_rows[:, 0, :, :]
            g_abs, g_sign = gabs[:, 0, :, :], gabs[:, 1, :, :]
            dve.tensor_scalar(g_sign, ga, 0.0, 2.0, ALU.is_ge, ALU.mult)
            step(dve.scalar_tensor_tensor(g_abs, ga, -1.0, ga, ALU.mult, ALU.max))
            step(dve.tensor_scalar(g_abs, g_abs, 0.25, None, ALU.max))
            step(dve.scalar_tensor_tensor(ga, g_sign, -1.0, g_abs, ALU.add, ALU.mult))

            dve.wait_ge(q["fold_ps"], 1)
            dve.tensor_copy(ab[:], bank_of(0)[0:HD, 0:2 * P].rearrange("p (a c) -> p a c", a=2)).then_inc(q["fold_c"], 1)
            dve.wait_ge(q["fold_ps"], 2)
            dve.wait_ge(q["tr_c"], len(turns))
            dve.wait_ge(q["ln_sd"], 1)
            f0, f1 = bank_of(1), bank_of(2)
            dve.tensor_tensor(wbias[:], wbias[:], f0[:, 3 * P:4 * P], ALU.add)
            dve.reciprocal(rstd[:], sdev[:])
            dve.tensor_copy(wp[:], f0[:, P:P + 2 * HD])
            dve.tensor_tensor(bp[:], f0[0:2 * HD, 2 * P:2 * P + 1], pred1b[:], ALU.add)
            dve.tensor_copy(gateWT[:], turned[:, 5, 0:E])
            for b in range(B):
                step(dve.tensor_copy(wrow[:, b, 2 * HD:2 * HD + MEM], f0[:, 0:MEM]))
                dve.tensor_tensor(wrow[:, b, P:2 * P], f1[:, 0:P], ga[:, b, :], ALU.mult)
                dve.tensor_tensor(wpr[0:2 * HD, b, :], f1[0:2 * HD, P:2 * P], ga[0:2 * HD, b, :], ALU.mult)
                dve.tensor_tensor(wpr[2 * HD:2 * HD + 1, b, :], wbias[2 * HD:2 * HD + 1, :], ga[2 * HD:2 * HD + 1, b, :], ALU.mult)
                for r in (0, 3):
                    rows = slice(HD * r, HD * r + HD)
                    dve.tensor_tensor(wcomb[rows, b, :], wb[rows, :], ga[rows, b, :], ALU.mult)
                for r in range(2):
                    last = dve.tensor_tensor(wcomb[HD * (r + 1):HD * (r + 2), b, :], f1[HD * r:HD * (r + 1), 2 * P:3 * P],
                                             ga[HD * r:HD * (r + 1), b, :], ALU.mult)
            last.then_inc(q["weights"], 1)

            def normalise(i, n, s):
                dve.wait_ge(q["a_tr"], n)
                for b in range(B):
                    t = i + NT * b
                    last = dve.tensor_scalar(xh[:, s, b, :], x_sb[:, t, :], col(mean, t), col(rstd, t), ALU.subtract, ALU.mult)
                last.then_inc(q["a_xh"], 1)

            def rows_out(i, n, s):
                dve.wait_ge(q["a_pb"], n + 2)
                ps = pb[2 + s]
                dve.tensor_copy(v_bt[:, :, i, :, 0:HD], ps[:, :, 0:2 * HD].rearrange("p b (h c) -> p b h c", h=2)).then_inc(q["a_ev"], 1)
                dve.tensor_copy(om_bt[:, :, i, HD:HD + MEM], ps[:, :, 2 * HD:2 * HD + MEM]).then_inc(q["a_ev"], 1)
                dve.tensor_tensor(x1_bt[:, :, i, :], x_bt[:, :, i, :], ps[:, :, P:2 * P], ALU.add).then_inc(q["a_ev"], 1)

            dve.wait_ge(q["filled"], 2)
            step(dve.tensor_copy(tick[:], ones[0:1, 0:1]))
            normalise(0, 1, 0)
            with dve.Fori(0, NT // 2 - 1) as i2:
                for s in range(2):
                    i = i2 * 2 + s
                    normalise(i + 1, i + 2, 1 - s)
                    rows_out(i, i + 1, s)
            normalise(NT - 1, NT, 1)
            for s in range(2):
                rows_out(NT - 2 + s, NT - 1 + s, s)

            dve.wait_ge(q["a_ev"], 3 * NT + 6)
            mem = om[:, :, HD:HD + MEM]
            step(dve.tensor_reduce(mstat[:, 0, :], mem, X, ALU.max))
            dve.tensor_tensor(mem, mem, mstat[:, 0, :].unsqueeze(2).to_broadcast([P, TT, MEM]), ALU.subtract).then_inc(q["mem_s"], 1)
            dve.wait_ge(q["mem_e"], 1)
            step(dve.tensor_reduce(mstat[:, 1, :], mem, X, ALU.add))
            step(dve.reciprocal(mstat[:, 2, :], mstat[:, 1, :]))
            dve.tensor_tensor(mem, mem, mstat[:, 2, :].unsqueeze(2).to_broadcast([P, TT, MEM]), ALU.mult).then_inc(q["mem_d"], 1)

            def scores_in(i, b, between=()):
                n = i * 2 + (b + 1)
                t = i + NT * b
                dve.wait_ge(q["b_sl"], n)
                dve.wait_ge(q["b_el"], n)
                dve.tensor_scalar(junk[:].rearrange("p (a c) -> p a c", a=2), pb[0][:, :, :], -SCALE, None, ALU.mult,
                                  ALU.min, accum_out=nml[:, b:b + 1]).then_inc(q["b_nm"], 1)
                for f in between:
                    f()
                dve.wait_ge(q["b_sc"], n + 2)
                dve.tensor_scalar(s_all[:, t, :].rearrange("p (a c) -> p a c", a=2), pb[1][:, :, :], SCALE, None,
                                  ALU.mult, ALU.max, accum_out=col(smax, t)).then_inc(q["b_se"], 1)
                dve.wait_ge(q["b_se"], n + 1)
                dve.tensor_scalar(col(snmax, t), col(smax, t), -1.0, None, ALU.mult).then_inc(q["b_sn"], 1)

            def local_out(i, b):
                n = i * 2 + (b + 1)
                dve.wait_ge(q["b_pv"], n + 2)
                dve.reciprocal(rl[:, b:b + 1], bank_of(6 + b)[:, HD:HD + 1]).then_inc(q["b_rl"], 1)
                dve.wait_ge(q["b_rl"], n)
                dve.tensor_scalar(om[:, i + NT * b, 0:HD], bank_of(6 + b)[:, 0:HD], rl[:, b:b + 1], None,
                                  ALU.mult).then_inc(q["b_no"], 1)

            AIM = KTOP - 8
            Z = normal_quantile(AIM / S)
            SIGMA = math.sqrt(math.pi / 2) / (S // 2)
            MOVE = math.sqrt(2 * math.pi) * math.exp(Z * Z / 2) / S
            DAMP = (1.0, 0.8, 0.6)

            def guess(t):
                dve.wait_ge(q["k_abs"], t + 1)
                dve.tensor_scalar(kstep[:], kabs[:], -0.5 * MOVE * SIGMA, None, ALU.mult)
                dve.tensor_scalar(col(kneg, t * 4), kabs[:], -Z * SIGMA, None, ALU.mult).then_inc(q["k_up"], 1)

            def move(t, r):
                dve.wait_ge(q["k_cnt"], t * 3 + (r + 1))
                dve.wait_ge(q["k_up"], t * 4 + (r + 2))
                dve.tensor_scalar(kmove[:], ksum[:], float(S - 2 * AIM), kstep[:, 0:1], ALU.add, ALU.mult).then_inc(q["k_u"], 1)
                dve.wait_ge(q["k_u"], t * 3 + (r + 1))
                dve.scalar_tensor_tensor(col(kneg, t * 4 + (r + 1)), kmove[:], DAMP[r], col(kneg, t * 4 + r), ALU.mult,
                                         ALU.add).then_inc(q["k_up"], 1)
                if r == 2:
                    dve.wait_ge(q["k_up"], t * 4 + 5)
                    dve.tensor_scalar(kguess[:], col(kneg, t * 4 + 3), -1.0, None, ALU.mult).then_inc(q["k_th"], 1)

            def below(t):
                dve.wait_ge(q["k_th"], t + 1)
                dve.tensor_scalar(junk[:], s_all[:, t, :], kguess[:, 0:1], None, ALU.is_ge, ALU.add, accum_out=kcount[:])

            def keep(t):
                dve.scalar_tensor_tensor(kwork[:], s_all[:, t, :], kguess[:, 0:1], s_all[:, t, :], ALU.is_lt,
                                         ALU.mult).then_inc(q["k_y"], 1)

            def eight(t, half):
                dve.wait_ge(q["k_y" if half == 0 else "k_r"], t + 1)
                dve.memset(tick[:], 0.0)
                dve.max(k16[:, 8 * half:8 * half + 8], kwork[:]).then_inc(q["k_m1" if half == 0 else "k_m2"], 1)

            def strike(t):
                dve.wait_ge(q["k_m1"], t + 1)
                dve.memset(tick[:], 0.0)
                dve.match_replace(kwork[:], k16[:, 0:8], kwork[:], NEG).then_inc(q["k_r"], 1)

            def threshold(t):
                dve.wait_ge(q["k_m2"], t + 1)
                dve.scalar_tensor_tensor(kpick[:], krank[:], kcount[:, 0:1], k16[:], ALU.is_equal, ALU.mult,
                                         accum_out=col(thr, t)).then_inc(q["thr_r"], 1)

            def full_search(b):
                dve.wait_ge(q["thr_r"], NT * (b + 1))
                dve.tensor_scalar(kpick[:, 0:NT], thr[:, NT * b:NT * (b + 1)], 0.0, None, ALU.is_gt, ALU.add,
                                  accum_out=kfound[:]).then_inc(q["k_good"], 1)
                dve.wait_ge(q["k_sum"], b + 1)
                dve.tensor_scalar(kflag[:], bank_of(7)[0:1, 511:512], -1.0, float(S), ALU.mult, ALU.add).then_inc(q["k_flag"], 1)
                dve.wait_ge(q["k_flag"], b + 1)
                missing = dve.value_load(kflag[0:1, 0:1], min_val=0, max_val=S)
                slow, STEPS = q[f"k_slow{b}"], 2 * ROUNDS
                with dve.If(missing):
                    with dve.Fori(0, NT) as i:
                        dve.tensor_copy(kwork[:], s_all[:, i + NT * b, :]).then_inc(slow, 1)
                        for r in range(ROUNDS):
                            dve.wait_ge(slow, i * STEPS + (2 * r + 1))
                            dve.memset(tick[:], 0.0)
                            dve.max(k8[:], kwork[:]).then_inc(slow, 1)
                            dve.wait_ge(slow, i * STEPS + (2 * r + 2))
                            if r < ROUNDS - 1:
                                dve.memset(tick[:], 0.0)
                                dve.match_replace(kwork[:], k8[:], kwork[:], NEG).then_inc(slow, 1)
                            else:
                                last = (KTOP - 1) % 8
                                dve.tensor_copy(col(thr, i + NT * b), k8[:, last:last + 1])
                    dve.drain()

            def scores_and_search(i, t):
                scores_in(i, 0, [lambda: guess(t)] if t is not None else [])
                if t is not None:
                    move(t, 0)
                scores_in(i, 1, [lambda: move(t, 1)] if t is not None else [])
                if t is not None:
                    move(t, 2)
                    below(t)
                    keep(t)
                    eight(t, 0)
                local_out(i, 0)
                if t is not None:
                    strike(t)
                    eight(t, 1)
                local_out(i, 1)
                if t is not None:
                    threshold(t)

            scores_and_search(0, None)
            with dve.Fori(1, NT) as i:
                scores_and_search(i, i - 1)

            def search(t):
                guess(t)
                for r in range(3):
                    move(t, r)
                below(t)
                keep(t)
                eight(t, 0)
                strike(t)
                eight(t, 1)
                threshold(t)

            search(NT - 1)

            def sparse_mask(m, s):
                dve.wait_ge(q["t_e"], m + 2)
                dve.scalar_tensor_tensor(el[:, s, :], s_all[:, m - 1, :], col(thr, m - 1), el[:, s, :], ALU.is_ge,
                                         ALU.mult).then_inc(q["t_p"], 1)

            def sparse_out(m, s):
                dve.wait_ge(q["t_pv"], m + 2)
                dve.reciprocal(rs[:, s:s + 1], bank_of(6 + s)[:, HD:HD + 1]).then_inc(q["t_rs"], 1)
                dve.wait_ge(q["t_rs"], m)
                dve.wait_ge(q["t_ct"], m)
                dve.tensor_scalar(cs[:, s, HD + MEM:P], bank_of(6 + s)[:, 0:HD], rs[:, s:s + 1], None, ALU.mult).then_inc(q["t_no"], 1)

            def residual(m, s):
                dve.wait_ge(q["t_xm"], m + 2)
                dve.tensor_tensor(x1[:, m - 1, :], x1[:, m - 1, :], bank_of(6 + s)[:, 2 * P:3 * P], ALU.add).then_inc(q["t_x1"], 1)
                dve.wait_ge(q["t_x1"], m + 2)
                dve.bn_stats(stats[:, m - 1, :], x1[:, m - 1, :]).then_inc(q["t_st"], 1)

            def stage(b, k, s, parts="mor"):
                m = k + (NT * b + 1)
                if "m" in parts:
                    sparse_mask(m, s)
                if "o" in parts:
                    sparse_out(m - 1, 1 - s)
                if "r" in parts:
                    residual(m - 2, s)

            def sparse_tail(b):
                stage(b, 0, 0, "m")
                stage(b, 1, 1, "mo")
                with dve.Fori(1, NT // 2) as i2:
                    for s in range(2):
                        stage(b, i2 * 2 + s, s)
                stage(b, NT, 0, "or")
                stage(b, NT + 1, 1, "r")

            def second_norm(b):
                dve.wait_ge(q["t_st"], NT * (b + 1))
                aggregate(NT * b, NT, 1e-5).then_inc(q["h_st"], 1)
                dve.wait_ge(q["h_sd"], b + 1)
                dve.reciprocal(rstd[:, 0:NT], sdev[:, 0:NT]).then_inc(q["h_rs"], 1)
                dve.wait_ge(q["h_rs"], b + 1)
                with dve.Fori(0, NT // 2) as i2:
                    for s in range(2):
                        t = i2 * 2 + s
                        dve.wait_ge(q["h_tr"], i2 * 2 + (NT * b + s + 1))
                        dve.tensor_scalar(xh[:, s, 0, :], x1[:, t + NT * b, :], col(mean, t), col(rstd, t), ALU.subtract,
                                          ALU.mult).then_inc(q["h_xh"], 1)
                dve.wait_ge(q["h_lg"], NT * (b + 1) + 2)
                lps = bank_of(6)[:, 0:NT * E].rearrange("p (t e) -> p t e", e=E)
                step(dve.tensor_reduce(g1[:], lps, X, ALU.max))
                dve.tensor_tensor(lg[:], lps, g1[:].unsqueeze(2).to_broadcast([P, NT, E]), ALU.subtract).then_inc(q["g_sub"], 1)

            def softmax_gates(b):
                dve.wait_ge(q["g_exp"], b + 1)
                step(dve.tensor_reduce(g1[:], gates[:], X, ALU.add))
                step(dve.reciprocal(g1[:], g1[:]))
                step(dve.tensor_tensor(gates[:], gates[:], g1[:].unsqueeze(2).to_broadcast([P, NT, E]), ALU.mult))

            def compare_gates():
                mine = gates[:].unsqueeze(3).to_broadcast([P, NT, E, E])
                other = gates[:].unsqueeze(2).to_broadcast([P, NT, E, E])
                dve.tensor_tensor(cmp1, other, mine, ALU.is_gt)
                step(dve.tensor_tensor(cmp2, other, mine, ALU.is_equal))

            def break_ties():
                step(dve.tensor_tensor(cmp2.rearrange("p t e j -> p t (e j)"), cmp2.rearrange("p t e j -> p t (e j)"),
                                       earlier[:].rearrange("p e j -> p (e j)").unsqueeze(1).to_broadcast([P, NT, E * E]), ALU.mult))

            def rank_gates():
                step(dve.tensor_tensor(cmp1, cmp1, cmp2, ALU.add))
                step(dve.tensor_reduce(rank[:], cmp1, X, ALU.add))

            def select_gates():
                step(dve.tensor_scalar(rank[:], rank[:], 2.0, 0.5, ALU.is_lt, ALU.mult))
                step(dve.tensor_tensor(gates[:], gates[:], rank[:], ALU.mult))

            def chunk(place, k):
                n = place * (NG * FC) + (k + 1)
                dve.wait_ge(q["f_sg"], n + 2)
                dve.tensor_tensor(gu[k // FC][:, k % FC, :], silu[:, k % 2, :], bank_of(2 + k % 2), ALU.mult).then_inc(q["f_gu"], 1)

            def weigh(place, g, gate):
                dve.wait_ge(q["f_dn"], place * NG + (g + 3))
                dve.wait_ge(q["f_ac"], place * (NG * TG) + TG * (g + 1))
                for j in range(TG):
                    t = TG * g + j
                    dve.scalar_tensor_tensor(acc[:, t, :], bank_of(4 + g)[:, j * P:(j + 1) * P], gate(t), acc[:, t, :],
                                             ALU.mult, ALU.add).then_inc(q["f_ac"], 1)

            def experts(b):
                dve.wait_ge(q["acc0"], b + 1)
                place = (E + 1) * b
                gating = [lambda: softmax_gates(b), compare_gates, break_ties, rank_gates, select_gates]
                for k in range(NG * FC):
                    chunk(place, k)
                    if 1 <= k <= len(gating):
                        gating[k - 1]()
                for g in range(NG):
                    weigh(place, g, lambda t: 0.5 / NS)
                with dve.Fori(0, E) as e:
                    place = e + ((E + 1) * b + 1)
                    t = e + NT
                    for k in range(NG * FC):
                        chunk(place, k)
                        if b == 0 and k == 1:
                            guess(t)
                        if b == 0 and k in (3, 5, 7):
                            move(t, (k - 3) // 2)
                    if b == 0:
                        below(t)
                    weigh(place, 0, lambda t: gates[:, t, bass.ds(e, 1)])
                    if b == 0:
                        keep(t)
                        eight(t, 0)
                        strike(t)
                    weigh(place, 1, lambda t: gates[:, t, bass.ds(e, 1)])
                    if b == 0:
                        eight(t, 1)
                        threshold(t)
                dve.wait_ge(q["f_ac"], (E + 1) * (b + 1) * (NG * TG) + 8)
                dve.wait_ge(q["gb_done"], 5)
                step(dve.tensor_tensor(acc[:], acc[:], gate_rows[:, 1, b, :].unsqueeze(1).to_broadcast([P, NT, P]), ALU.mult))
                own = x1[:, NT * b:NT * b + NT, :]
                dve.tensor_tensor(own, own, acc[:], ALU.add).then_inc(q["o_add"], 1)

            for b in range(B):
                full_search(b)
                sparse_tail(b)
                second_norm(b)
                experts(b)

        @block.tensor
        def _(pe):
            for name in ("a_tr", "a_pa", "a_pb", "b_sc", "b_tr", "b_pv", "t_tr", "t_pv", "t_ct", "t_xm", "h_tr", "h_lg",
                         "f_up", "f_dn"):
                pe.sem_inc(q[name], 2)

            def product(out, lhsT, rhs, start=True, stop=True):
                return pe.matmul(out, lhsT, rhs, start=start, stop=stop)

            pe.wait_ge(q["cst"], 4)
            pe.wait_ge(q["l_small"], ALL_SMALL)
            for j, (src, rows) in enumerate(turns):
                n = src.shape[0]
                last = pe.transpose(bank_of(4 + j // 4)[0:rows, (j % 4) * P:(j % 4) * P + n], src, ident[0:n, 0:n])
            last.then_inc(q["tr_w"], 1)

            pe.wait_ge(q["c_silu"], 1)
            pe.wait_ge(q["l_wmod"], 16)
            for j, k in enumerate((0, 1, 3, 4)):
                product(bank_of(6)[:, B * j:B * j + B], wmod[:, k * P:(k + 1) * P], siluc[:])
            for j, k in enumerate((2, 5)):
                for b in range(B):
                    last = product(bank_of(7)[:, (B * j + b) * P:(B * j + b + 1) * P], silub[:, b, :], wmod[:, k * P:(k + 1) * P])
            last.then_inc(q["m_ps"], 1)

            pe.wait_ge(q["c_silu"], 2)
            pe.wait_ge(q["tr_c"], len(turns))
            projT, predinT, bankT, memoutT, pred2T = (turned[0:HD, j, :] for j in range(5))
            for r in range(2):
                last = product(bank_of(0)[0:HD, r * P:(r + 1) * P], memoutT[:, HD * r:HD * (r + 1)], wb_mem[:])
            last.then_inc(q["fold_ps"], 1)
            f0, f1 = bank_of(1), bank_of(2)
            product(f0[:, 0:MEM], projT, bankT[:, 0:MEM])
            product(f0[:, P:P + 2 * HD], predinT, pred1[:])
            product(f0[0:2 * HD, 2 * P:2 * P + 1], pred1[:], bcols[:, 2:3])
            product(f0[:, 3 * P:4 * P], bwide[:, 0, :], wb_mem[:], True, False)
            product(f0[:, 3 * P:4 * P], bwide[:, 1, :], wb_pred[:], False, True)
            product(f1[0:2 * HD, P:2 * P], pred2T[:, 0:2 * HD], wb_pred[:])
            pe.wait_ge(q["fold_c"], 1)
            product(f1[:, 0:P], projT, ab[:, 0, :])
            product(f1[0:MEM, 2 * P:3 * P], bankT[:, 0:MEM], ab[:, 1, :]).then_inc(q["fold_ps"], 1)

            def transposed(n, s):
                pe.wait_ge(q["a_xh"], n + 2)
                pe.wait_ge(q["a_hs"], n)
                for b in range(B):
                    last = pe.transpose(bank_of(s)[:, b * P:(b + 1) * P], xh[:, s, b, :], ident[:])
                last.then_inc(q["a_tr"], 1)

            def projections(n, s):
                pe.wait_ge(q["a_hs"], n + 2)
                pe.wait_ge(q["a_qk"], n * 2)
                pe.wait_ge(q["a_ev"], n * 3)
                both = hs[:, s, :, :].rearrange("p b d -> p (b d)")
                product(bank_of(2 + s)[0:2 * HD, 2 * P:4 * P], wp[:], both)
                product(bank_of(2 + s)[:, 0:2 * P], wqk[:].rearrange("p k c -> p (k c)"), both).then_inc(q["a_pa"], 1)
                for b in range(B):
                    product(pb[2 + s][:, b, 0:2 * P], hs[:, s, b, :], wrow[:, b, :], True, False)
                pe.wait_ge(q["a_gl"], n + 1)
                for b in range(B):
                    last = product(pb[2 + s][:, b, P:2 * P], gelu[:, b, :], wpr[:, b, :], False, True)
                last.then_inc(q["a_pb"], 1)

            pe.wait_ge(q["weights"], 1)
            transposed(1, 0)
            with pe.Fori(0, NT // 2 - 1) as i2:
                for s in range(2):
                    n = i2 * 2 + (s + 1)
                    transposed(n + 1, 1 - s)
                    projections(n, s)
            transposed(NT, 1)
            for s in range(2):
                projections(NT - 1 + s, s)

            pe.wait_ge(q["a_qk"], 2 * NT + 4)
            pe.wait_ge(q["a_ev"], 3 * NT + 6)

            def scores(i, b):
                n = i * 2 + (b + 1)
                pe.wait_ge(q["b_qs"], n + 2)
                pe.wait_ge(q["b_el"], n + 1)
                for half in range(2):
                    keys = slice(NT * b + 4 * half, NT * b + 4 * half + 4)
                    last = product(pb[0][:, half, :], qs[0:HD, b, :], qk[0:HD, keys, 1, :])
                last.then_inc(q["b_sl"], 1)
                pe.wait_ge(q["b_se"], n)
                for half in range(2):
                    keys = slice(NT * b + 4 * half, NT * b + 4 * half + 4)
                    last = product(pb[1][:, half, :], qs[HD:2 * HD, b, :], qk[HD:2 * HD, keys, 1, :])
                last.then_inc(q["b_sc"], 1)

            def turn(banks, probs):
                for c in range(NT):
                    last = pe.transpose(banks[:, c // 4, (c % 4) * P:(c % 4 + 1) * P], probs[:, c * P:(c + 1) * P], ident[:])
                return last

            def weighted(out, slot, b, head):
                for c in range(NT):
                    last = product(out[:, 0:HD + 1], et[:, slot, c, :], v[:, NT * b + c, head, :], c == 0, c == NT - 1)
                return last

            def local(i, b):
                n = i * 2 + (b + 1)
                pe.wait_ge(q["b_el"], n + 2)
                pe.wait_ge(q["b_ev"], n)
                turn(pb[2], el[:, b, :]).then_inc(q["b_tr"], 1)
                pe.wait_ge(q["b_ev"], n + 1)
                pe.wait_ge(q["b_no"], n)
                weighted(bank_of(6 + b), b, b, 0).then_inc(q["b_pv"], 1)

            with pe.Fori(0, NT) as i:
                for b in range(B):
                    scores(i, b)
                for b in range(B):
                    local(i, b)

            def stage(b, k, s, parts="tpc"):
                m = k + (NT * b + 1)
                if "t" in parts:
                    pe.wait_ge(q["t_p"], m + 2)
                    pe.wait_ge(q["t_ev"], m)
                    turn(pb[2 - s], el[:, s, :]).then_inc(q["t_tr"], 1)
                if "c" in parts:
                    pe.wait_ge(q["t_cs"], m)
                    pe.wait_ge(q["t_no"], m)
                    pe.transpose(bank_of(6 + s)[:, P:2 * P], cs[:, s, :], ident[:]).then_inc(q["t_ct"], 1)
                if "p" in parts:
                    pe.wait_ge(q["t_ev"], m + 1)
                    pe.wait_ge(q["t_x1"], m - 1)
                    weighted(bank_of(7 - s), 1 - s, b, 1).then_inc(q["t_pv"], 1)
                if "c" in parts:
                    pe.wait_ge(q["t_cc"], m)
                    product(bank_of(6 + s)[:, 2 * P:3 * P], csT[:, s, :], wcomb[:, b, :]).then_inc(q["t_xm"], 1)

            def rows_found(b):
                pe.wait_ge(q["k_good"], b + 1)
                pe.wait_ge(q["b_no"], TT + 2)
                product(bank_of(7)[0:1, 511:512], kfound[:], ones[:, 0:1]).then_inc(q["k_sum"], 1)

            def sparse_tail(b):
                stage(b, 0, 0, "t")
                stage(b, 1, 1, "tp")
                with pe.Fori(1, NT // 2) as i2:
                    for s in range(2):
                        stage(b, i2 * 2 + s, s)
                stage(b, NT, 0, "pc")
                stage(b, NT + 1, 1, "c")

            def second_norm(b):
                with pe.Fori(0, NT // 2) as i2:
                    for s in range(2):
                        n = i2 * 2 + (NT * b + s + 1)
                        pe.wait_ge(q["h_xh"], n + 2)
                        pe.wait_ge(q["h_hs"], n)
                        pe.transpose(bank_of(s)[:, 0:P], xh[:, s, 0, :], ident[:]).then_inc(q["h_tr"], 1)
                        pe.wait_ge(q["h_hs"], n + 2)
                        product(bank_of(6)[:, bass.ds((i2 * 2 + s) * E, E)], hs[:, s, 0, :], gateWT[:]).then_inc(q["h_lg"], 1)
                pe.wait_ge(q["h_cp"], NT * (b + 1) + 2)

            def expert(ex, up, down):
                for g in range(NG):
                    for c in range(FC):
                        pe.wait_ge(q["f_gu"], ex * (NG * FC) + (FC * g + c + 1))
                        for j in range(2):
                            last = product(bank_of(2 * j + c % 2), up(j)[:, c * P:(c + 1) * P], h2T[:, g * GRP:(g + 1) * GRP])
                        last.then_inc(q["f_up"], 1)
                for g in range(NG):
                    pe.wait_ge(q["f_gu"], ex * (NG * FC) + (FC * (g + 1) + 2))
                    pe.wait_ge(q["f_ac"], ex * (NG * TG) + TG * (g + 1))
                    for j in range(TG):
                        for c in range(FC):
                            last = product(bank_of(4 + g)[:, j * P:(j + 1) * P], gu[g][:, c, j * P:(j + 1) * P], down[:, c, :],
                                           c == 0, c == FC - 1)
                    last.then_inc(q["f_dn"], 1)

            def experts(b):
                pe.wait_ge(q["l_ws"], 48)
                expert((E + 1) * b, lambda j: w13s[:, j, :], w2s)
                with pe.Fori(0, E // 2) as e2:
                    for s in range(2):
                        pe.wait_ge(l_w[s], e2 * 48 + 48 * (E // 2 * b + 1))
                        expert(e2 * 2 + (s + (E + 1) * b + 1), lambda j: w13[:, s, j, :], w2[:, s, :, :])

            for b in range(B):
                rows_found(b)
                if b > 0:
                    pe.wait_ge(q["f_ac"], (E + 1) * NG * TG + 8)
                sparse_tail(b)
                second_norm(b)
                experts(b)


_INS = ['L0_attn_x', 'L0_attn_local_qkv_w', 'L0_attn_sparse_qkv_w', 'L0_attn_memory_bank', 'L0_attn_memory_proj_w',
        'L0_attn_mem_out_w', 'L0_attn_mem_out_b', 'L0_attn_pred_in_w', 'L0_attn_pred_in_b', 'L0_attn_pred1_w',
        'L0_attn_pred1_b', 'L0_attn_pred2_w', 'L0_attn_pred2_b', 'L0_attn_warboss_w', 'L0_attn_warboss_b',
        'L0_ffn_gate_W', 'L0_ffn_w1_e', 'L0_ffn_w3_e', 'L0_ffn_w2_e', 'L0_ffn_w1_s', 'L0_ffn_w3_s', 'L0_ffn_w2_s',
        'L0_c', 'L0_wmod']


def kernel(**inputs):
    import numpy as _np
    import concourse.bacc as _bacc
    from concourse import mybir as _mybir
    from concourse.bass_utils import run_bass_kernel_spmd as _run

    nc = _bacc.Bacc("TRN2", target_bir_lowering=False, num_devices=1)
    arrays, io = {}, {}
    for name in _INS:
        a = _np.ascontiguousarray(inputs[name])
        arrays[f"in_{name}_dram"] = a
        io[name] = nc.dram_tensor(f"in_{name}_dram", a.shape, _mybir.dt.from_np(a.dtype), kind="ExternalInput").ap()
    io["out"] = nc.dram_tensor("out_0_dram", inputs["L0_attn_x"].shape, _mybir.dt.float32, kind="ExternalOutput").ap()
    build(nc, io)
    r = _run(nc, [arrays], core_ids=[0])
    return r.results[0]["out_0_dram"]
```

```python
import math
from contextlib import ExitStack

import concourse.bass as bass
from concourse import mybir

F32 = mybir.dt.float32
BF16 = mybir.dt.bfloat16
ALU = mybir.AluOpType
ACT = mybir.ActivationFunctionType
X = mybir.AxisListType.X

P = 128
NEG = -3.0e38


def normal_quantile(tail):
    low, high = 0.0, 8.0
    for _ in range(60):
        mid = (low + high) / 2
        low, high = (mid, high) if math.erfc(mid / math.sqrt(2)) / 2 > tail else (low, mid)
    return low


def build(nc, io):
    x_d, out_d = io["L0_attn_x"], io["out"]
    B, S, D = x_d.shape
    HD = io["L0_attn_memory_bank"].shape[1]
    MEM = io["L0_attn_memory_bank"].shape[0]
    E, _, F = io["L0_ffn_w1_e"].shape
    NS, _, FS = io["L0_ffn_w1_s"].shape
    NT = S // P
    TT = B * NT
    FC = F // P
    KTOP = max(1, int(S * 0.1))
    ROUNDS = (KTOP + 7) // 8
    SCALE = HD ** -0.5
    GRP = 512
    NG = S // GRP
    TG = GRP // P
    assert B == 2 and D == P and NS * FS == F and HD == 32 and MEM == 64 and E == NT

    ctx = ExitStack()
    with ctx:
        def sb(name, shape, dt=F32):
            return ctx.enter_context(nc.sbuf_tensor(name, shape, dt))

        def sem(name):
            return ctx.enter_context(nc.semaphore(name))

        ident = sb("ident", [P, P])
        ones = sb("ones", [P, P])
        earlier = sb("earlier", [P, E, E])
        cT = sb("cT", [P, B])
        sig = sb("sig", [P, 2, B])
        siluc = sb("siluc", [P, B])
        silub = sb("silub", [P, B, P])
        wmod = sb("wmod", [P, 6 * P])
        mcol = sb("mcol", [P, 4, B])
        gate_rows = sb("gate_rows", [P, 2, B, P])
        wqk = sb("wqk", [P, 2, 2 * HD])
        wrow = sb("wrow", [P, B, 2 * P])
        proj = sb("proj", [P, HD])
        predin = sb("predin", [P, HD])
        bank = sb("bank", [MEM, HD])
        memout = sb("memout", [2 * HD, HD])
        pred2 = sb("pred2", [2 * HD, HD])
        gateW = sb("gateW", [E, P])
        gateWT = sb("gateWT", [P, E])
        pred1 = sb("pred1", [HD, 2 * HD])
        pred1b = sb("pred1b", [2 * HD, 1])
        bcols = sb("bcols", [HD, 3])
        bwide = sb("bwide", [HD, 2, P])
        wb = sb("wb", [P, P])
        wb_mem = sb("wb_mem", [HD, P])
        wb_pred = sb("wb_pred", [HD, P])
        wbias = sb("wbias", [P, P])
        turned = sb("turned", [P, 6, P])
        ab = sb("ab", [HD, 2, P])
        wp = sb("wp", [P, 2 * HD])
        bp = sb("bp", [2 * HD, 1])
        wcomb = sb("wcomb", [P, B, P])
        wpr = sb("wpr", [2 * HD + 1, B, P])
        x_sb = sb("x_sb", [P, TT, P])
        x1 = sb("x1", [P, TT, P])
        stats = sb("stats", [P, TT, 6])
        mean = sb("mean", [P, TT])
        var = sb("var", [P, TT])
        sdev = sb("sdev", [P, TT])
        rstd = sb("rstd", [P, TT])
        lt = sb("lt", [P, 2, TT])
        xh = sb("xh", [P, 2, B, P])
        hs = sb("hs", [P, 2, B, P])
        qk = sb("qk", [P, TT, P])
        gelu = sb("gelu", [2 * HD + 1, B, P])
        v = sb("v", [P, TT, 2, HD + 1])
        om = sb("om", [P, TT, HD + MEM])
        mstat = sb("mstat", [P, 3, TT])
        xhat = xh[:].rearrange("p s b d -> p (s b) d")
        qs = sb("qs", [P, B, 2, P])
        s_all = sb("s_all", [P, TT, S])
        v_bt = v[:].rearrange("p (b t) h c -> p b t h c", b=B)
        om_bt = om[:].rearrange("p (b t) c -> p b t c", b=B)
        x1_bt = x1[:].rearrange("p (b t) d -> p b t d", b=B)
        x_bt = x_sb[:].rearrange("p (b t) d -> p b t d", b=B)
        qk_bt = qk[:].rearrange("p (b t) d -> p b t d", b=B)
        smax = sb("smax", [P, TT])
        snmax = sb("snmax", [P, TT])
        thr = sb("thr", [P, TT])
        junk = sb("junk", [P, S], BF16)
        nml = sb("nml", [P, 2])
        el = sb("el", [P, 2, S])
        et = sb("et", [P, 2, NT, P])
        rl = sb("rl", [P, 2])
        rs = sb("rs", [P, 2])
        kwork = sb("kwork", [P, S])
        k8 = sb("k8", [P, 8])
        k16 = sb("k16", [P, 16])
        krank = sb("krank", [P, 16])
        kpick = sb("kpick", [P, 16])
        ajunk = sb("ajunk", [P, S], BF16)
        kabs = sb("kabs", [P, 1])
        kstep = sb("kstep", [P, 1])
        ksum = sb("ksum", [P, 1])
        kmove = sb("kmove", [P, 1])
        kneg = sb("kneg", [P, 4 * TT])
        kguess = sb("kguess", [P, 1])
        kcount = sb("kcount", [P, TT])
        kfound = sb("kfound", [P, 1])
        kflag = sb("kflag", [1, 1], mybir.dt.int32)
        pool_tick = sb("pool_tick", [1, 1])
        tick = sb("tick", [1, 1])
        gabs = kwork[:, 0:S // 2].rearrange("p (k b d) -> p k b d", k=2, b=B)
        cs = sb("cs", [P, 2, P])
        csT = sb("csT", [P, 2, P])
        h2T = sb("h2T", [P, S])
        lg = sb("lg", [P, NT, E])
        g1 = sb("g1", [P, NT])
        cmp1, cmp2 = (kwork[:, h * S // 2:(h + 1) * S // 2].rearrange("p (t e j) -> p t e j", t=NT, e=E) for h in range(2))
        rank = sb("rank", [P, NT, E])
        gates = sb("gates", [P, NT, E])
        w13 = sb("w13", [P, 2, 2, F])
        w2 = sb("w2", [P, 2, FC, P])
        w13s = sb("w13s", [P, 2, F])
        w13b = sb("w13b", [P, 2, 2, 2, F], BF16)
        w13sb = sb("w13sb", [P, 2, 2, F], BF16)
        h2b = sb("h2b", [P, 2, S], BF16)
        w2s = sb("w2s", [P, FC, P])
        silu = sb("silu", [P, 3, GRP])
        gu = [el[:, :, :].rearrange("p a (c t) -> p (a c) t", t=GRP),
              sb("gu1", [P, FC, GRP])]
        acc = x_sb[:, 0:NT, :]

        pb = [ctx.enter_context(nc.psum_tensor(f"pb{n}", [P, 2, 512], F32)) for n in range(4)]

        def bank_of(n):
            return pb[n // 2][:, n % 2, :]

        names = """l_c l_x l_wmod l_small l_pool l_w0 l_w1 l_ws cst filled acc0 c_exp c_silu m_ps gb_raw gb_done
        tr_w tr_c fold_ps fold_c weights ln_st ln_sd
        a_xh a_tr a_hs a_pa a_qk a_gl a_pb a_ev mem_s mem_e mem_d
        qs0 b_qs b_sl b_sc b_nm b_se b_sn b_el b_tr b_ev b_pv b_rl b_no
        k_abs k_cnt k_up k_u k_th k_y k_m1 k_r k_m2 thr_r k_good k_sum k_flag k_slow0 k_slow1
        t_e t_p t_tr t_ev t_pv t_rs t_no t_cs t_ct t_cc t_xm t_x1 t_st
        h_st h_sd h_rs h_xh h_tr h_hs h_hi h_lo h_lg s_hi s_lo w_hi w_lo g_sub g_exp
        f_up f_sg f_gu f_dn f_ac o_add out_done dve_step""".split()
        q = {n: sem(n) for n in names}
        l_w = [q["l_w0"], q["l_w1"]]

        x_v = x_d.rearrange("b (t p) d -> p (b t) d", p=P)
        out_v = out_d.rearrange("b (t p) d -> p (b t) d", p=P)
        w1_d, w3_d, w2_d = io["L0_ffn_w1_e"], io["L0_ffn_w3_e"], io["L0_ffn_w2_e"]

        def column(a):
            return a.rearrange("(a b) -> a b", b=1)

        wlo, wsp, wbo = io["L0_attn_local_qkv_w"], io["L0_attn_sparse_qkv_w"], io["L0_attn_warboss_w"]
        small = [(proj[:], io["L0_attn_memory_proj_w"]), (predin[:], io["L0_attn_pred_in_w"]),
                 (bank[:], io["L0_attn_memory_bank"]), (memout[:], io["L0_attn_mem_out_w"]),
                 (pred2[:], io["L0_attn_pred2_w"]), (gateW[:], io["L0_ffn_gate_W"]),
                 (pred1[:], io["L0_attn_pred1_w"])]
        for k, w in enumerate((wlo, wsp)):
            small += [(wqk[:, :, HD * k:HD * k + HD], w[:, 0:2 * HD].rearrange("p (k d) -> p k d", k=2))]
            small += [(wrow[:, b, HD * k:HD * k + HD], w[:, 2 * HD:3 * HD]) for b in range(B)]
        small += [(wb[0:HD, :], wbo[0:HD, :]), (wb[3 * HD:4 * HD, :], wbo[HD:2 * HD, :]),
                  (wb_mem[:], wbo[2 * HD:3 * HD, :]), (wb_pred[:], wbo[3 * HD:4 * HD, :]),
                  (wbias[:], io["L0_attn_warboss_b"].partition_broadcast(P)),
                  (pred1b[:], column(io["L0_attn_pred1_b"])), (bcols[:, 0:1], column(io["L0_attn_mem_out_b"])),
                  (bcols[:, 1:2], column(io["L0_attn_pred2_b"])), (bcols[:, 2:3], column(io["L0_attn_pred_in_b"]))]
        SMALL_POOL = 16 * len(small[2::3])
        SMALL_REST = 16 * len(small) - SMALL_POOL

        def col(t, n):
            return t[:, n:n + 1] if isinstance(n, int) else t[:, bass.ds(n, 1)]

        gate_bank, up_bank = (0, 1, 6), (2, 3, 7)

        def slot_freed(place, k):
            return place * (NG * FC) + max(k, 2)

        turns = [(proj[:], HD), (predin[:], HD), (bank[:], HD), (memout[:], HD), (pred2[:], HD), (gateW[:], P)]

        block = ctx.enter_context(nc.Block())

        @block.sync
        def _(sp):
            for b in range(B):
                sp.dma_start(cT[:, b:b + 1], column(io["L0_c"][b])).then_inc(q["l_c"], 16)
            for b in range(B):
                sp.dma_start(x_sb[:, NT * b:NT * b + NT, :], x_v[:, NT * b:NT * b + NT, :]).then_inc(q["l_x"], 16)
            for dst, src in small[0::3]:
                sp.dma_start(dst, src).then_inc(q["l_small"], 16)

            def load_expert(e, s):
                for j, w in enumerate((w1_d, w3_d)):
                    sp.dma_start(w13[:, s, j, :], w[e]).then_inc(l_w[s], 16)
                sp.dma_start(w2[:, s, :, :], w2_d[e].rearrange("(c p) d -> p c d", p=P)).then_inc(l_w[s], 16)

            for s in range(2):
                load_expert(s, s)
            for j, w in enumerate((io["L0_ffn_w1_s"], io["L0_ffn_w3_s"])):
                sp.dma_start(w13s[:, j, :].rearrange("p (n f) -> p n f", n=NS),
                             w.rearrange("n d f -> d n f")).then_inc(q["l_ws"], 16)
            sp.dma_start(w2s[:], io["L0_ffn_w2_s"].rearrange("n f d -> (n f) d")
                         .rearrange("(c p) d -> p c d", p=P)).then_inc(q["l_ws"], 16)
            for b in range(B):
                for s in range(2):
                    if b > 0:
                        sp.wait_ge(q["f_dn"], NG * ((E + 1) * b - 2 + s + 1) + 2)
                        load_expert(s, s)
                with sp.Fori(1, E // 2) as e2:
                    for s in range(2):
                        sp.wait_ge(q["f_dn"], e2 * (2 * NG) + (NG * s + 2 + NG * (E + 1) * b))
                        load_expert(e2 * 2 + s, s)
            for b in range(B):
                sp.wait_ge(q["o_add"], b + 1)
                sp.dma_start(out_v[:, NT * b:NT * b + NT, :], x1[:, NT * b:NT * b + NT, :]).then_inc(q["out_done"], 16)
            sp.wait_ge(q["out_done"], 16 * B)

        @block.gpsimd
        def _(pool):
            for dst, src in small[2::3]:
                pool.dma_start(dst, src).then_inc(q["l_pool"], 16)
            for name in ("b_qs", "t_cs"):
                pool.sem_inc(q[name], 2)
            pool.memset(ones[:], 1.0).then_inc(q["cst"], 1)
            pool.wait_ge(q["cst"], 1)
            pool.affine_select(out=ident[:], in_=ones[:], pattern=[[-1, P]], compare_op=ALU.is_equal, fill=0.0,
                               base=0, channel_multiplier=1).then_inc(q["cst"], 1)
            pool.affine_select(out=earlier[:], in_=ones[:, 0:E * E].rearrange("p (e j) -> p e j", e=E),
                               pattern=[[1, E], [-1, E]], compare_op=ALU.is_gt, fill=0.0,
                               base=0, channel_multiplier=0).then_inc(q["cst"], 1)
            pool.iota(krank[:], pattern=[[-2, 16]], base=2 * (KTOP - 1) - S, channel_multiplier=0,
                      allow_small_or_imprecise_dtypes=True).then_inc(q["cst"], 1)
            pool.memset(gelu[:], 1.0).then_inc(q["filled"], 1)
            pool.memset(v[:], 1.0).then_inc(q["filled"], 1)

            pool.wait_ge(q["gb_raw"], 1)
            gb = gate_rows[:, 1, :, :]
            g_abs, g_sign = csT[:], cs[:]
            pool.tensor_scalar(g_sign, gb, 0.0, 2.0, ALU.is_ge, ALU.mult).then_inc(q["gb_done"], 1)
            pool.wait_ge(q["gb_done"], 1)
            pool.tensor_scalar(g_sign, g_sign, -1.0, None, ALU.add).then_inc(q["gb_done"], 1)
            pool.wait_ge(q["gb_done"], 2)
            pool.tensor_tensor(g_abs, g_sign, gb, ALU.mult).then_inc(q["gb_done"], 1)
            pool.wait_ge(q["gb_done"], 3)
            pool.tensor_scalar(g_abs, g_abs, 0.25, None, ALU.max).then_inc(q["gb_done"], 1)
            pool.wait_ge(q["gb_done"], 4)
            pool.tensor_tensor(gb, g_abs, g_sign, ALU.mult).then_inc(q["gb_done"], 1)

            def split(n, slot):
                pool.tensor_copy(w13b[:, slot, 0, :, :], w13[:, slot, :, :]).then_inc(q["w_hi"], 1)
                pool.wait_ge(q["w_hi"], n)
                pool.tensor_tensor(w13b[:, slot, 1, :, :], w13[:, slot, :, :], w13b[:, slot, 0, :, :],
                                   ALU.subtract).then_inc(q["w_lo"], 1)

            pool.wait_ge(q["l_ws"], 48)
            pool.tensor_copy(w13sb[:, 0, :, :], w13s[:]).then_inc(q["s_hi"], 1)
            pool.wait_ge(q["s_hi"], 1)
            pool.tensor_tensor(w13sb[:, 1, :, :], w13s[:], w13sb[:, 0, :, :], ALU.subtract).then_inc(q["s_lo"], 1)
            for s in range(2):
                pool.wait_ge(l_w[s], 48)
                split(s + 1, s)

            pool.memset(qs[:], 0.0).then_inc(q["qs0"], 1)
            pool.wait_ge(q["qs0"], 1)
            pool.wait_ge(q["a_qk"], NT + 2)
            with pool.Fori(0, NT) as i:
                for b in range(B):
                    pool.wait_ge(q["b_sc"], i * 2 + (b + 1))
                    for head in range(2):
                        last = pool.tensor_copy(qs[HD * (2 + head):HD * (3 + head), b, head, :],
                                                qk[HD * head:HD * (head + 1), i + NT * b, :])
                    last.then_inc(q["b_qs"], 1)

            def combined_slot(m, s):
                pool.wait_ge(q["t_ct"], m)
                pool.tensor_copy(cs[:, s, 0:HD + MEM], om[:, m - 1, :]).then_inc(q["t_cs"], 1)

            def sparse_tail(b):
                with pool.Fori(0, NT // 2) as i2:
                    for s in range(2):
                        combined_slot(i2 * 2 + (NT * b + s + 1), s)

            def split_rest(b):
                with pool.Fori(1, E // 2) as e2:
                    for s in range(2):
                        pool.wait_ge(l_w[s], e2 * 48 + 48 * (E // 2 * b + 1))
                        pool.wait_ge(q["f_up"], e2 * (2 * NG * FC) + (NG * FC * ((E + 1) * b + s) + 2))
                        pool.tensor_tensor(pool_tick[:], ones[0:1, 0:1], ones[0:1, 0:1], ALU.mult)
                        split(e2 * 2 + (E * b + s + 1), s)
                if b < B - 1:
                    for s in range(2):
                        pool.wait_ge(l_w[s], 48 * (E // 2 * (b + 1) + 1))
                        pool.wait_ge(q["f_up"], NG * FC * ((E + 1) * b + E + s) + 2)
                        split(E * (b + 1) + s + 1, s)

            pool.wait_ge(q["b_no"], TT + 2)
            pool.memset(acc, 0.0).then_inc(q["acc0"], 1)
            pool.wait_ge(q["mem_d"], 1)
            sparse_tail(0)
            split_rest(0)
            sparse_tail(1)
            pool.wait_ge(q["o_add"], 1)
            pool.memset(acc, 0.0).then_inc(q["acc0"], 1)
            split_rest(1)

        @block.scalar
        def _(act):
            act.dma_start(wmod[:], io["L0_wmod"]).then_inc(q["l_wmod"], 16)
            for dst, src in small[1::3]:
                act.dma_start(dst, src).then_inc(q["l_small"], 16)
            for name, n in (("a_hs", 2), ("a_qk", 2), ("a_gl", 1), ("b_el", 2), ("b_ev", 1), ("t_e", 2), ("t_ev", 2),
                            ("t_cc", 2), ("f_sg", 2), ("k_cnt", 1)):
                act.sem_inc(q[name], n)

            act.wait_ge(q["l_c"], 16 * B)
            act.activation(sig[:, 0, :], cT[:], ACT.Exp, scale=-1.0).then_inc(q["c_exp"], 1)
            act.wait_ge(q["ln_st"], 1)
            act.activation(sdev[:], var[:], ACT.Sqrt).then_inc(q["ln_sd"], 1)
            act.preload_act_table(ACT.Gelu)
            act.wait_ge(q["tr_w"], 1)
            for j, (src, rows) in enumerate(turns):
                n = src.shape[0]
                act.copy(turned[0:rows, j, 0:n], bank_of(4 + j // 4)[0:rows, (j % 4) * P:(j % 4) * P + n]).then_inc(q["tr_c"], 1)

            def first_h(n, s):
                act.wait_ge(q["a_tr"], n + 2)
                act.wait_ge(q["a_pb"], n)
                for b in range(B):
                    last = act.activation(hs[:, s, b, :], bank_of(s)[:, b * P:(b + 1) * P], ACT.Identity,
                                          scale=mcol[:, 1, b:b + 1], bias=mcol[:, 0, b:b + 1])
                last.then_inc(q["a_hs"], 1)

            def pair_out(i, n, s):
                act.wait_ge(q["a_pa"], n + 2)
                act.wait_ge(q["a_pb"], n + 1)
                pair = bank_of(2 + s).rearrange("p (k b d) -> p k b d", k=2, b=B)
                act.activation(gelu[0:2 * HD, :, :], pair[0:2 * HD, 1, :, :], ACT.Gelu, bias=bp[:, 0:1]).then_inc(q["a_gl"], 1)
                act.copy(qk_bt[:, :, i, :], pair[:, 0, :, :]).then_inc(q["a_qk"], 1)

            act.wait_ge(q["weights"], 1)
            act.wait_ge(q["filled"], 1)
            first_h(1, 0)
            with act.Fori(0, NT // 2 - 1) as i2:
                for s in range(2):
                    i = i2 * 2 + s
                    first_h(i + 2, 1 - s)
                    pair_out(i, i + 1, s)
            first_h(NT, 1)
            for s in range(2):
                pair_out(NT - 2 + s, NT - 1 + s, s)

            act.preload_act_table(ACT.Exp)

            def local_exp(i, b):
                n = i * 2 + (b + 1)
                act.wait_ge(q["b_nm"], n + 2)
                act.wait_ge(q["b_tr"], n)
                act.activation(el[:, b, :].rearrange("p (a c) -> p a c", a=2), pb[0][:, :, :], ACT.Exp, scale=SCALE,
                               bias=nml[:, b:b + 1]).then_inc(q["b_el"], 1)

            def turned_local(i, b):
                n = i * 2 + (b + 1)
                act.wait_ge(q["b_tr"], n + 2)
                act.wait_ge(q["b_pv"], n)
                act.copy(et[:, b, :, :].rearrange("p (a c) q -> p a (c q)", a=2), pb[2][:, :, :]).then_inc(q["b_ev"], 1)

            def spread(t):
                act.wait_ge(q["k_up"], t * 4 + 1)
                act.wait_ge(q["k_cnt"], t * 4 + 1)
                act.activation(ajunk[:, 0:S // 2], s_all[:, t, 0:S // 2], ACT.Abs, accum_out=kabs[:]).then_inc(q["k_abs"], 1)

            def count(t, r):
                act.wait_ge(q["k_up"], t * 4 + (r + 2))
                act.activation(ajunk[:], s_all[:, t, :], ACT.Sign, bias=col(kneg, t * 4 + r),
                               accum_out=col(kcount, t) if r == 3 else ksum[:]).then_inc(q["k_cnt"], 1)

            local_exp(0, 0)
            act.wait_ge(q["mem_s"], 1)
            act.activation(om[:, :, HD:HD + MEM], om[:, :, HD:HD + MEM], ACT.Exp).then_inc(q["mem_e"], 1)
            local_exp(0, 1)
            turned_local(0, 0)
            with act.Fori(1, NT) as i:
                act.wait_ge(q["b_sn"], i * 2 - 1)
                spread(i - 1)
                local_exp(i, 0)
                count(i - 1, 0)
                turned_local(i - 1, 1)
                count(i - 1, 1)
                local_exp(i, 1)
                count(i - 1, 2)
                turned_local(i, 0)
                count(i - 1, 3)
            turned_local(NT - 1, 1)
            act.wait_ge(q["b_sn"], TT)
            spread(NT - 1)
            for r in range(4):
                count(NT - 1, r)

            def sparse_exp(m, s):
                act.wait_ge(q["t_tr"], m)
                act.activation(el[:, s, :], s_all[:, m - 1, :], ACT.Exp, bias=col(snmax, m - 1)).then_inc(q["t_e"], 1)

            def turned_sparse(m, s):
                act.wait_ge(q["t_tr"], m + 2)
                act.wait_ge(q["t_pv"], m)
                act.copy(et[:, s, :, :].rearrange("p (a c) q -> p a (c q)", a=2), pb[2 - s][:, :, :]).then_inc(q["t_ev"], 1)

            def combined_copy(m, s):
                act.wait_ge(q["t_ct"], m + 2)
                act.wait_ge(q["t_xm"], m)
                act.copy(csT[:, s, :], bank_of(6 + s)[:, P:2 * P]).then_inc(q["t_cc"], 1)

            def stage(b, k, s, parts="tce"):
                m = k + (NT * b + 1)
                if "t" in parts:
                    turned_sparse(m, s)
                if "c" in parts:
                    combined_copy(m - 2, s)
                if "e" in parts:
                    sparse_exp(m + 2, s)

            def sparse_tail(b):
                stage(b, -2, 0, "e")
                stage(b, -1, 1, "e")
                stage(b, 0, 0, "te")
                stage(b, 1, 1, "te")
                with act.Fori(1, NT // 2 - 1) as i2:
                    for s in range(2):
                        stage(b, i2 * 2 + s, s)
                stage(b, NT - 2, 0, "tc")
                stage(b, NT - 1, 1, "tc")
                stage(b, NT, 0, "c")
                stage(b, NT + 1, 1, "c")

            def second_norm(b):
                act.wait_ge(q["h_st"], b + 1)
                act.activation(sdev[:, 0:NT], var[:, 0:NT], ACT.Sqrt).then_inc(q["h_sd"], 1)
                for g in range(NG):
                    act.wait_ge(q["h_tr"], NT * b + TG * (g + 1))
                    act.activation(h2T[:, g * GRP:(g + 1) * GRP], bank_of(g), ACT.Identity, scale=mcol[:, 3, b:b + 1],
                                   bias=mcol[:, 2, b:b + 1]).then_inc(q["h_hs"], 1)
                    act.activation(h2b[:, 0, g * GRP:(g + 1) * GRP], bank_of(g), ACT.Identity, scale=mcol[:, 3, b:b + 1],
                                   bias=mcol[:, 2, b:b + 1]).then_inc(q["h_hi"], 1)
                act.wait_ge(q["g_sub"], b + 1)
                act.activation(gates[:], lg[:], ACT.Exp).then_inc(q["g_exp"], 1)
                act.preload_act_table(ACT.Silu)

            def expert(place, t=None):
                for k in range(NG * FC):
                    n = place * (NG * FC) + (k + 1)
                    act.wait_ge(q["f_up"], n + 2)
                    act.wait_ge(q["f_gu"], slot_freed(place, k))
                    act.activation(silu[:, k % 3, :], bank_of(gate_bank[k % 3]), ACT.Silu).then_inc(q["f_sg"], 1)
                    if t is not None:
                        if k == 0:
                            spread(t)
                        if k in (2, 4, 6, 7):
                            count(t, (2, 4, 6, 7).index(k))

            def experts(b):
                if b < B - 1:
                    expert(0, NT)
                    with act.Fori(1, E) as e:
                        expert(e, e + NT)
                    expert(E)
                else:
                    with act.Fori(0, E + 1) as e:
                        expert(e + (E + 1) * b)

            for b in range(B):
                sparse_tail(b)
                second_norm(b)
                experts(b)
                if b == 0:
                    act.preload_act_table(ACT.Exp)
                    act.wait_ge(q["f_dn"], (E + 1) * NG + 2)

        @block.vector
        def _(dve):
            for name, n in (("a_xh", 2), ("a_ev", 6), ("b_nm", 2), ("b_se", 1), ("b_no", 2), ("t_p", 2), ("t_no", 2),
                            ("t_x1", 2), ("f_gu", 2), ("f_ac", 8), ("k_up", 1), ("thr_r", 1)):
                dve.sem_inc(q[name], n)
            steps = [0]

            def step(ins):
                steps[0] += 1
                ins.then_inc(q["dve_step"], 1)
                dve.wait_ge(q["dve_step"], steps[0])

            def aggregate(t0, n, eps):
                st = stats[:, t0:t0 + n, :]
                step(dve.tensor_tensor(mean[:, 0:n], st[:, :, 1], st[:, :, 4], ALU.add))
                step(dve.tensor_tensor(lt[:, 0, 0:n], st[:, :, 1], st[:, :, 4], ALU.subtract))
                step(dve.tensor_tensor(lt[:, 1, 0:n], st[:, :, 2], st[:, :, 5], ALU.add))
                step(dve.tensor_tensor(lt[:, 0, 0:n], lt[:, 0, 0:n], lt[:, 0, 0:n], ALU.mult))
                step(dve.scalar_tensor_tensor(lt[:, 1, 0:n], lt[:, 0, 0:n], P / 4.0, lt[:, 1, 0:n], ALU.mult, ALU.add))
                step(dve.tensor_scalar(mean[:, 0:n], mean[:, 0:n], 0.5, None, ALU.mult))
                return dve.tensor_scalar(var[:, 0:n], lt[:, 1, 0:n], 1.0 / P, eps, ALU.mult, ALU.add)

            dve.wait_ge(q["c_exp"], 1)
            dve.wait_ge(q["cst"], 4)
            step(dve.tensor_scalar(sig[:, 1, :], sig[:, 0, :], 1.0, None, ALU.add))
            step(dve.reciprocal(sig[:, 0, :], sig[:, 1, :]))
            step(dve.tensor_tensor(siluc[:], cT[:], sig[:, 0, :], ALU.mult))
            for b in range(B):
                last = dve.tensor_scalar(silub[:, b, :], ones[:], siluc[:, b:b + 1], None, ALU.mult)
            last.then_inc(q["c_silu"], 1)
            dve.wait_ge(q["l_x"], 16 * B)
            for t in range(TT):
                last = dve.bn_stats(stats[:, t, :], x_sb[:, t, :])
            step(last)
            aggregate(0, TT, 1e-5).then_inc(q["ln_st"], 1)
            dve.wait_ge(q["l_small"], SMALL_REST)
            dve.wait_ge(q["l_pool"], SMALL_POOL)
            for j in range(2):
                last = dve.tensor_scalar(bwide[:, j, :], ones[0:HD, :], bcols[:, j:j + 1], None, ALU.mult)
            last.then_inc(q["c_silu"], 1)

            dve.wait_ge(q["m_ps"], 1)
            mps = bank_of(6)[:, 0:4 * B].rearrange("p (k b) -> p k b", k=4)
            for k in range(4):
                dve.tensor_scalar(mcol[:, k, :], mps[:, k, :], float(k % 2), None, ALU.add)
            gps = bank_of(7).rearrange("p (k b d) -> p k b d", k=2, b=B)
            step(dve.tensor_copy(gate_rows[:], gps))
            dve.tensor_copy(tick[:], ones[0:1, 0:1]).then_inc(q["gb_raw"], 1)
            ga = gate_rows[:, 0, :, :]
            g_abs, g_sign = gabs[:, 0, :, :], gabs[:, 1, :, :]
            dve.tensor_scalar(g_sign, ga, 0.0, 2.0, ALU.is_ge, ALU.mult)
            step(dve.scalar_tensor_tensor(g_abs, ga, -1.0, ga, ALU.mult, ALU.max))
            step(dve.tensor_scalar(g_abs, g_abs, 0.25, None, ALU.max))
            step(dve.scalar_tensor_tensor(ga, g_sign, -1.0, g_abs, ALU.add, ALU.mult))

            dve.wait_ge(q["fold_ps"], 1)
            dve.tensor_copy(ab[:], bank_of(0)[0:HD, 0:2 * P].rearrange("p (a c) -> p a c", a=2)).then_inc(q["fold_c"], 1)
            dve.wait_ge(q["fold_ps"], 2)
            dve.wait_ge(q["tr_c"], len(turns))
            dve.wait_ge(q["ln_sd"], 1)
            f0, f1 = bank_of(1), bank_of(2)
            dve.tensor_tensor(wbias[:], wbias[:], f0[:, 3 * P:4 * P], ALU.add)
            dve.reciprocal(rstd[:], sdev[:])
            dve.tensor_copy(wp[:], f0[:, P:P + 2 * HD])
            dve.tensor_tensor(bp[:], f0[0:2 * HD, 2 * P:2 * P + 1], pred1b[:], ALU.add)
            dve.tensor_copy(gateWT[:], turned[:, 5, 0:E])
            for b in range(B):
                step(dve.tensor_copy(wrow[:, b, 2 * HD:2 * HD + MEM], f0[:, 0:MEM]))
                dve.tensor_tensor(wrow[:, b, P:2 * P], f1[:, 0:P], ga[:, b, :], ALU.mult)
                dve.tensor_tensor(wpr[0:2 * HD, b, :], f1[0:2 * HD, P:2 * P], ga[0:2 * HD, b, :], ALU.mult)
                dve.tensor_tensor(wpr[2 * HD:2 * HD + 1, b, :], wbias[2 * HD:2 * HD + 1, :], ga[2 * HD:2 * HD + 1, b, :], ALU.mult)
                for r in (0, 3):
                    rows = slice(HD * r, HD * r + HD)
                    dve.tensor_tensor(wcomb[rows, b, :], wb[rows, :], ga[rows, b, :], ALU.mult)
                for r in range(2):
                    last = dve.tensor_tensor(wcomb[HD * (r + 1):HD * (r + 2), b, :], f1[HD * r:HD * (r + 1), 2 * P:3 * P],
                                             ga[HD * r:HD * (r + 1), b, :], ALU.mult)
            last.then_inc(q["weights"], 1)

            def normalise(i, n, s):
                dve.wait_ge(q["a_tr"], n)
                for b in range(B):
                    t = i + NT * b
                    last = dve.tensor_scalar(xh[:, s, b, :], x_sb[:, t, :], col(mean, t), col(rstd, t), ALU.subtract, ALU.mult)
                last.then_inc(q["a_xh"], 1)

            def rows_out(i, n, s):
                dve.wait_ge(q["a_pb"], n + 2)
                ps = pb[2 + s]
                dve.tensor_copy(v_bt[:, :, i, :, 0:HD], ps[:, :, 0:2 * HD].rearrange("p b (h c) -> p b h c", h=2)).then_inc(q["a_ev"], 1)
                dve.tensor_copy(om_bt[:, :, i, HD:HD + MEM], ps[:, :, 2 * HD:2 * HD + MEM]).then_inc(q["a_ev"], 1)
                dve.tensor_tensor(x1_bt[:, :, i, :], x_bt[:, :, i, :], ps[:, :, P:2 * P], ALU.add).then_inc(q["a_ev"], 1)

            dve.wait_ge(q["filled"], 2)
            step(dve.tensor_copy(tick[:], ones[0:1, 0:1]))
            for s in range(2):
                normalise(s, s + 1, s)
            with dve.Fori(0, NT // 2 - 1) as i2:
                for s in range(2):
                    i = i2 * 2 + s
                    normalise(i + 2, i + 3, s)
                    rows_out(i, i + 1, s)
            for s in range(2):
                rows_out(NT - 2 + s, NT - 1 + s, s)

            mem = om[:, :, HD:HD + MEM]

            def memory_shift():
                step(dve.tensor_reduce(mstat[:, 0, :], mem, X, ALU.max))
                dve.tensor_tensor(mem, mem, mstat[:, 0, :].unsqueeze(2).to_broadcast([P, TT, MEM]), ALU.subtract).then_inc(q["mem_s"], 1)

            def memory_weights():
                dve.wait_ge(q["mem_e"], 1)
                step(dve.tensor_reduce(mstat[:, 1, :], mem, X, ALU.add))
                step(dve.reciprocal(mstat[:, 2, :], mstat[:, 1, :]))
                dve.tensor_tensor(mem, mem, mstat[:, 2, :].unsqueeze(2).to_broadcast([P, TT, MEM]), ALU.mult).then_inc(q["mem_d"], 1)

            def local_out(i, b):
                n = i * 2 + (b + 1)
                dve.wait_ge(q["b_pv"], n + 2)
                dve.reciprocal(rl[:, b:b + 1], bank_of(6 + b)[:, HD:HD + 1]).then_inc(q["b_rl"], 1)
                dve.wait_ge(q["b_rl"], n)
                dve.tensor_scalar(om[:, i + NT * b, 0:HD], bank_of(6 + b)[:, 0:HD], rl[:, b:b + 1], None,
                                  ALU.mult).then_inc(q["b_no"], 1)

            AIM = KTOP - 8
            Z = normal_quantile(AIM / S)
            SIGMA = math.sqrt(math.pi / 2) / (S // 2)
            MOVE = math.sqrt(2 * math.pi) * math.exp(Z * Z / 2) / S
            DAMP = (1.0, 0.8, 0.6)

            def guess(t):
                dve.wait_ge(q["k_abs"], t + 1)
                dve.tensor_scalar(kstep[:], kabs[:], -0.5 * MOVE * SIGMA, None, ALU.mult)
                dve.tensor_scalar(col(kneg, t * 4), kabs[:], -Z * SIGMA, None, ALU.mult).then_inc(q["k_up"], 1)

            def move(t, r):
                dve.wait_ge(q["k_cnt"], t * 4 + (r + 2))
                dve.wait_ge(q["k_up"], t * 4 + (r + 2))
                dve.tensor_scalar(kmove[:], ksum[:], float(S - 2 * AIM), kstep[:, 0:1], ALU.add, ALU.mult).then_inc(q["k_u"], 1)
                dve.wait_ge(q["k_u"], t * 3 + (r + 1))
                dve.scalar_tensor_tensor(col(kneg, t * 4 + (r + 1)), kmove[:], DAMP[r], col(kneg, t * 4 + r), ALU.mult,
                                         ALU.add).then_inc(q["k_up"], 1)

            def keep(t):
                dve.wait_ge(q["k_up"], t * 4 + 5)
                dve.tensor_scalar(kguess[:], col(kneg, t * 4 + 3), -1.0, None, ALU.mult).then_inc(q["k_th"], 1)
                dve.wait_ge(q["k_th"], t + 1)
                dve.scalar_tensor_tensor(kwork[:], s_all[:, t, :], kguess[:, 0:1], s_all[:, t, :], ALU.is_lt,
                                         ALU.mult).then_inc(q["k_y"], 1)

            def eight(t, half):
                dve.wait_ge(q["k_y" if half == 0 else "k_r"], t + 1)
                dve.memset(tick[:], 0.0)
                dve.max(k16[:, 8 * half:8 * half + 8], kwork[:]).then_inc(q["k_m1" if half == 0 else "k_m2"], 1)

            def strike(t):
                dve.wait_ge(q["k_m1"], t + 1)
                dve.memset(tick[:], 0.0)
                dve.match_replace(kwork[:], k16[:, 0:8], kwork[:], NEG).then_inc(q["k_r"], 1)

            def threshold(t):
                dve.wait_ge(q["k_cnt"], t * 4 + 5)
                dve.wait_ge(q["k_m2"], t + 1)
                dve.scalar_tensor_tensor(kpick[:], krank[:], col(kcount, t), k16[:], ALU.is_equal, ALU.mult,
                                         accum_out=col(thr, t)).then_inc(q["thr_r"], 1)

            def full_search(b):
                dve.wait_ge(q["thr_r"], NT * (b + 1) + 1)
                dve.tensor_scalar(kpick[:, 0:NT], thr[:, NT * b:NT * (b + 1)], 0.0, None, ALU.is_gt, ALU.add,
                                  accum_out=kfound[:]).then_inc(q["k_good"], 1)
                dve.wait_ge(q["k_sum"], b + 1)
                dve.tensor_scalar(kflag[:], bank_of(7)[0:1, 511:512], -1.0, float(S), ALU.mult, ALU.add).then_inc(q["k_flag"], 1)
                dve.wait_ge(q["k_flag"], b + 1)
                missing = dve.value_load(kflag[0:1, 0:1], min_val=0, max_val=S)
                slow, STEPS = q[f"k_slow{b}"], 2 * ROUNDS
                with dve.If(missing):
                    with dve.Fori(0, NT) as i:
                        dve.tensor_copy(kwork[:], s_all[:, i + NT * b, :]).then_inc(slow, 1)
                        for r in range(ROUNDS):
                            dve.wait_ge(slow, i * STEPS + (2 * r + 1))
                            dve.memset(tick[:], 0.0)
                            dve.max(k8[:], kwork[:]).then_inc(slow, 1)
                            dve.wait_ge(slow, i * STEPS + (2 * r + 2))
                            if r < ROUNDS - 1:
                                dve.memset(tick[:], 0.0)
                                dve.match_replace(kwork[:], k8[:], kwork[:], NEG).then_inc(slow, 1)
                            else:
                                last = (KTOP - 1) % 8
                                dve.tensor_copy(col(thr, i + NT * b), k8[:, last:last + 1])
                    dve.drain()

            def local_scores(i, b):
                n = i * 2 + (b + 1)
                dve.wait_ge(q["b_sl"], n)
                dve.wait_ge(q["b_el"], n)
                dve.tensor_scalar(junk[:].rearrange("p (a c) -> p a c", a=2), pb[0][:, :, :], -SCALE, None, ALU.mult,
                                  ALU.min, accum_out=nml[:, b:b + 1]).then_inc(q["b_nm"], 1)

            def sparse_scores(i, b):
                n = i * 2 + (b + 1)
                t = i + NT * b
                dve.wait_ge(q["b_sc"], n + 2)
                dve.tensor_scalar(s_all[:, t, :].rearrange("p (a c) -> p a c", a=2), pb[1][:, :, :], SCALE, None,
                                  ALU.mult, ALU.max, accum_out=col(smax, t)).then_inc(q["b_se"], 1)
                dve.wait_ge(q["b_se"], n + 1)
                dve.tensor_scalar(col(snmax, t), col(smax, t), -1.0, None, ALU.mult).then_inc(q["b_sn"], 1)

            def tile(i, kept=True):
                local_scores(i, 0)
                guess(i - 1)
                sparse_scores(i, 0)
                move(i - 1, 0)
                if kept:
                    keep(i - 2)
                    eight(i - 2, 0)
                local_out(i - 1, 0)
                local_scores(i, 1)
                move(i - 1, 1)
                sparse_scores(i, 1)
                move(i - 1, 2)
                if kept:
                    strike(i - 2)
                    eight(i - 2, 1)
                    threshold(i - 2)
                local_out(i - 1, 1)

            dve.wait_ge(q["a_ev"], 3 * NT + 6)
            local_scores(0, 0)
            sparse_scores(0, 0)
            memory_shift()
            local_scores(0, 1)
            sparse_scores(0, 1)
            memory_weights()
            tile(1, kept=False)
            with dve.Fori(2, NT) as i:
                tile(i)
            guess(NT - 1)
            for r in range(3):
                if r == 0:
                    local_out(NT - 1, 0)
                move(NT - 1, r)
                if r == 0:
                    keep(NT - 2)
                    eight(NT - 2, 0)
                if r == 1:
                    strike(NT - 2)
                    eight(NT - 2, 1)
                    threshold(NT - 2)
                    local_out(NT - 1, 1)
            keep(NT - 1)
            eight(NT - 1, 0)
            strike(NT - 1)
            eight(NT - 1, 1)
            threshold(NT - 1)

            def sparse_mask(m, s):
                dve.wait_ge(q["t_e"], m + 2)
                dve.scalar_tensor_tensor(el[:, s, :], s_all[:, m - 1, :], col(thr, m - 1), el[:, s, :], ALU.is_ge,
                                         ALU.mult).then_inc(q["t_p"], 1)

            def sparse_out(m, s):
                dve.wait_ge(q["t_pv"], m + 2)
                dve.reciprocal(rs[:, s:s + 1], bank_of(6 + s)[:, HD:HD + 1]).then_inc(q["t_rs"], 1)
                dve.wait_ge(q["t_rs"], m)
                dve.wait_ge(q["t_ct"], m)
                dve.tensor_scalar(cs[:, s, HD + MEM:P], bank_of(6 + s)[:, 0:HD], rs[:, s:s + 1], None, ALU.mult).then_inc(q["t_no"], 1)

            def residual(m, s):
                dve.wait_ge(q["t_xm"], m + 2)
                dve.tensor_tensor(x1[:, m - 1, :], x1[:, m - 1, :], bank_of(6 + s)[:, 2 * P:3 * P], ALU.add).then_inc(q["t_x1"], 1)
                dve.wait_ge(q["t_x1"], m + 2)
                dve.bn_stats(stats[:, m - 1, :], x1[:, m - 1, :]).then_inc(q["t_st"], 1)

            def stage(b, k, s, parts="mor"):
                m = k + (NT * b + 1)
                if "m" in parts:
                    sparse_mask(m + 1, 1 - s)
                if "o" in parts:
                    sparse_out(m - 1, 1 - s)
                if "r" in parts:
                    residual(m - 2, s)

            def sparse_tail(b):
                stage(b, -1, 1, "m")
                stage(b, 0, 0, "m")
                stage(b, 1, 1, "mo")
                with dve.Fori(1, NT // 2 - 1) as i2:
                    for s in range(2):
                        stage(b, i2 * 2 + s, s)
                stage(b, NT - 2, 0)
                stage(b, NT - 1, 1, "or")
                stage(b, NT, 0, "or")
                stage(b, NT + 1, 1, "r")

            def second_norm(b):
                dve.wait_ge(q["t_st"], NT * (b + 1))
                aggregate(NT * b, NT, 1e-5).then_inc(q["h_st"], 1)
                dve.wait_ge(q["h_sd"], b + 1)
                dve.reciprocal(rstd[:, 0:NT], sdev[:, 0:NT]).then_inc(q["h_rs"], 1)
                dve.wait_ge(q["h_rs"], b + 1)
                for t in range(NT):
                    if t >= TG:
                        dve.wait_ge(q["h_tr"], NT * b + t - TG + 1)
                    dve.tensor_scalar(xhat[:, t % TG, :], x1[:, t + NT * b, :], mean[:, t:t + 1], rstd[:, t:t + 1],
                                      ALU.subtract, ALU.mult).then_inc(q["h_xh"], 1)
                for g in range(NG):
                    own = slice(g * GRP, (g + 1) * GRP)
                    dve.wait_ge(q["h_hi"], NG * b + g + 1)
                    dve.tensor_tensor(h2b[:, 1, own], h2T[:, own], h2b[:, 0, own], ALU.subtract).then_inc(q["h_lo"], 1)
                dve.wait_ge(q["h_lg"], b + 1)
                lps = bank_of(6)[:, 0:NT * E].rearrange("p (t e) -> p t e", e=E)
                step(dve.tensor_reduce(g1[:], lps, X, ALU.max))
                dve.tensor_tensor(lg[:], lps, g1[:].unsqueeze(2).to_broadcast([P, NT, E]), ALU.subtract).then_inc(q["g_sub"], 1)

            def softmax_gates(b):
                dve.wait_ge(q["g_exp"], b + 1)
                step(dve.tensor_reduce(g1[:], gates[:], X, ALU.add))
                step(dve.reciprocal(g1[:], g1[:]))
                step(dve.tensor_tensor(gates[:], gates[:], g1[:].unsqueeze(2).to_broadcast([P, NT, E]), ALU.mult))

            def compare_gates():
                mine = gates[:].unsqueeze(3).to_broadcast([P, NT, E, E])
                other = gates[:].unsqueeze(2).to_broadcast([P, NT, E, E])
                dve.tensor_tensor(cmp1, other, mine, ALU.is_gt)
                step(dve.tensor_tensor(cmp2, other, mine, ALU.is_equal))

            def break_ties():
                step(dve.tensor_tensor(cmp2.rearrange("p t e j -> p t (e j)"), cmp2.rearrange("p t e j -> p t (e j)"),
                                       earlier[:].rearrange("p e j -> p (e j)").unsqueeze(1).to_broadcast([P, NT, E * E]), ALU.mult))

            def rank_gates():
                step(dve.tensor_tensor(cmp1, cmp1, cmp2, ALU.add))
                step(dve.tensor_reduce(rank[:], cmp1, X, ALU.add))

            def select_gates():
                step(dve.tensor_scalar(rank[:], rank[:], 2.0, 0.5, ALU.is_lt, ALU.mult))
                step(dve.tensor_tensor(gates[:], gates[:], rank[:], ALU.mult))

            def chunk(place, k):
                n = place * (NG * FC) + (k + 1)
                dve.wait_ge(q["f_sg"], n + 2)
                dve.tensor_tensor(gu[k // FC][:, k % FC, :], silu[:, k % 3, :], bank_of(up_bank[k % 3]), ALU.mult).then_inc(q["f_gu"], 1)

            def weigh(place, g, gate):
                dve.wait_ge(q["f_dn"], place * NG + (g + 3))
                dve.wait_ge(q["f_ac"], place * (NG * TG) + TG * (g + 1))
                for j in range(TG):
                    t = TG * g + j
                    dve.scalar_tensor_tensor(acc[:, t, :], bank_of(4 + g)[:, j * P:(j + 1) * P], gate(t), acc[:, t, :],
                                             ALU.mult, ALU.add).then_inc(q["f_ac"], 1)

            def experts(b):
                dve.wait_ge(q["acc0"], b + 1)
                place = (E + 1) * b
                gating = [lambda: softmax_gates(b), compare_gates, break_ties, rank_gates, select_gates]
                guesses = {1: guess, 3: lambda t: move(t, 0), 5: lambda t: move(t, 1), 7: lambda t: move(t, 2)}
                search = {2: keep, 4: lambda t: eight(t, 0), 6: strike}

                def expert(place, gate, guessed, sought):
                    for k in range(NG * FC):
                        chunk(place, k)
                        if guessed is not None and k in guesses:
                            guesses[k](guessed)
                        if sought is not None and k in search:
                            search[k](sought)
                    if sought is not None:
                        eight(sought, 1)
                        threshold(sought)
                    for g in range(NG):
                        weigh(place, g, gate)

                for k in range(NG * FC):
                    chunk(place, k)
                    if 1 <= k <= len(gating):
                        gating[k - 1]()
                    if b < B - 1 and k in guesses:
                        guesses[k](NT)
                for g in range(NG):
                    weigh(place, g, lambda t: 0.5 / NS)
                if b < B - 1:
                    with dve.Fori(0, E - 1) as e:
                        expert(e + 1, lambda t: gates[:, t, bass.ds(e, 1)], e + (NT + 1), e + NT)
                    expert(E, lambda t: gates[:, t, E - 1:E], None, TT - 1)
                else:
                    with dve.Fori(0, E) as e:
                        expert(e + (place + 1), lambda t: gates[:, t, bass.ds(e, 1)], None, None)
                dve.wait_ge(q["f_ac"], (E + 1) * (b + 1) * (NG * TG) + 8)
                dve.wait_ge(q["gb_done"], 5)
                step(dve.tensor_tensor(acc, acc, gate_rows[:, 1, b, :].unsqueeze(1).to_broadcast([P, NT, P]), ALU.mult))
                own = x1[:, NT * b:NT * b + NT, :]
                dve.tensor_tensor(own, own, acc, ALU.add).then_inc(q["o_add"], 1)

            for b in range(B):
                full_search(b)
                sparse_tail(b)
                second_norm(b)
                experts(b)

        @block.tensor
        def _(pe):
            for name in ("a_tr", "a_pa", "a_pb", "b_sc", "b_tr", "b_pv", "t_tr", "t_pv", "t_ct", "t_xm",
                         "f_up", "f_dn"):
                pe.sem_inc(q[name], 2)

            def product(out, lhsT, rhs, start=True, stop=True):
                return pe.matmul(out, lhsT, rhs, start=start, stop=stop)

            pe.wait_ge(q["cst"], 4)
            pe.wait_ge(q["l_small"], SMALL_REST)
            pe.wait_ge(q["l_pool"], SMALL_POOL)
            for j, (src, rows) in enumerate(turns):
                n = src.shape[0]
                last = pe.transpose(bank_of(4 + j // 4)[0:rows, (j % 4) * P:(j % 4) * P + n], src, ident[0:n, 0:n])
            last.then_inc(q["tr_w"], 1)

            pe.wait_ge(q["c_silu"], 1)
            pe.wait_ge(q["l_wmod"], 16)
            for j, k in enumerate((0, 1, 3, 4)):
                product(bank_of(6)[:, B * j:B * j + B], wmod[:, k * P:(k + 1) * P], siluc[:])
            for j, k in enumerate((2, 5)):
                for b in range(B):
                    last = product(bank_of(7)[:, (B * j + b) * P:(B * j + b + 1) * P], silub[:, b, :], wmod[:, k * P:(k + 1) * P])
            last.then_inc(q["m_ps"], 1)

            pe.wait_ge(q["c_silu"], 2)
            pe.wait_ge(q["tr_c"], len(turns))
            projT, predinT, bankT, memoutT, pred2T = (turned[0:HD, j, :] for j in range(5))
            for r in range(2):
                last = product(bank_of(0)[0:HD, r * P:(r + 1) * P], memoutT[:, HD * r:HD * (r + 1)], wb_mem[:])
            last.then_inc(q["fold_ps"], 1)
            f0, f1 = bank_of(1), bank_of(2)
            product(f0[:, 0:MEM], projT, bankT[:, 0:MEM])
            product(f0[:, P:P + 2 * HD], predinT, pred1[:])
            product(f0[0:2 * HD, 2 * P:2 * P + 1], pred1[:], bcols[:, 2:3])
            product(f0[:, 3 * P:4 * P], bwide[:, 0, :], wb_mem[:], True, False)
            product(f0[:, 3 * P:4 * P], bwide[:, 1, :], wb_pred[:], False, True)
            product(f1[0:2 * HD, P:2 * P], pred2T[:, 0:2 * HD], wb_pred[:])
            pe.wait_ge(q["fold_c"], 1)
            product(f1[:, 0:P], projT, ab[:, 0, :])
            product(f1[0:MEM, 2 * P:3 * P], bankT[:, 0:MEM], ab[:, 1, :]).then_inc(q["fold_ps"], 1)

            def transposed(n, s):
                pe.wait_ge(q["a_xh"], n + 2)
                pe.wait_ge(q["a_hs"], n)
                for b in range(B):
                    last = pe.transpose(bank_of(s)[:, b * P:(b + 1) * P], xh[:, s, b, :], ident[:])
                last.then_inc(q["a_tr"], 1)

            def projections(n, s):
                pe.wait_ge(q["a_hs"], n + 2)
                pe.wait_ge(q["a_qk"], n)
                pe.wait_ge(q["a_ev"], n * 3)
                both = hs[:, s, :, :].rearrange("p b d -> p (b d)")
                product(bank_of(2 + s)[0:2 * HD, 2 * P:4 * P], wp[:], both)
                product(bank_of(2 + s)[:, 0:2 * P], wqk[:].rearrange("p k c -> p (k c)"), both).then_inc(q["a_pa"], 1)
                for b in range(B):
                    product(pb[2 + s][:, b, 0:2 * P], hs[:, s, b, :], wrow[:, b, :], True, False)
                pe.wait_ge(q["a_gl"], n + 1)
                for b in range(B):
                    last = product(pb[2 + s][:, b, P:2 * P], gelu[:, b, :], wpr[:, b, :], False, True)
                last.then_inc(q["a_pb"], 1)

            pe.wait_ge(q["weights"], 1)
            transposed(1, 0)
            with pe.Fori(0, NT // 2 - 1) as i2:
                for s in range(2):
                    n = i2 * 2 + (s + 1)
                    transposed(n + 1, 1 - s)
                    projections(n, s)
            transposed(NT, 1)
            for s in range(2):
                projections(NT - 1 + s, s)

            pe.wait_ge(q["a_qk"], NT + 2)
            pe.wait_ge(q["a_ev"], 3 * NT + 6)

            def local_scores(i, b):
                n = i * 2 + (b + 1)
                pe.wait_ge(q["b_qs"], n + 2)
                pe.wait_ge(q["b_el"], n + 1)
                for half in range(2):
                    keys = slice(NT * b + 4 * half, NT * b + 4 * half + 4)
                    last = product(pb[0][:, half, :], qs[:, b, 0, :], qk[:, keys, :])
                last.then_inc(q["b_sl"], 1)

            def sparse_scores(i, b):
                n = i * 2 + (b + 1)
                pe.wait_ge(q["b_se"], n)
                for half in range(2):
                    keys = slice(NT * b + 4 * half, NT * b + 4 * half + 4)
                    last = product(pb[1][:, half, :], qs[:, b, 1, :], qk[:, keys, :])
                last.then_inc(q["b_sc"], 1)

            def turn(banks, probs):
                for c in range(NT):
                    last = pe.transpose(banks[:, c // 4, (c % 4) * P:(c % 4 + 1) * P], probs[:, c * P:(c + 1) * P], ident[:])
                return last

            def weighted(out, slot, b, head):
                for c in range(NT):
                    last = product(out[:, 0:HD + 1], et[:, slot, c, :], v[:, NT * b + c, head, :], c == 0, c == NT - 1)
                return last

            def local_turn(i, b):
                n = i * 2 + (b + 1)
                pe.wait_ge(q["b_el"], n + 2)
                pe.wait_ge(q["b_ev"], n)
                turn(pb[2], el[:, b, :]).then_inc(q["b_tr"], 1)

            def local_product(i, b):
                n = i * 2 + (b + 1)
                pe.wait_ge(q["b_ev"], n + 1)
                pe.wait_ge(q["b_no"], n)
                weighted(bank_of(6 + b), b, b, 0).then_inc(q["b_pv"], 1)

            def tile(i, before=True, after=True):
                sparse_scores(i, 0)
                if before:
                    local_turn(i - 1, 1)
                    local_product(i - 1, 0)
                local_scores(i, 1)
                sparse_scores(i, 1)
                local_turn(i, 0)
                if before:
                    local_product(i - 1, 1)
                if after:
                    local_scores(i + 1, 0)

            local_scores(0, 0)
            tile(0, before=False)
            with pe.Fori(1, NT - 1) as i:
                tile(i)
            tile(NT - 1, after=False)
            local_turn(NT - 1, 1)
            for b in range(B):
                local_product(NT - 1, b)

            def stage(b, k, s, parts="tpc"):
                m = k + (NT * b + 1)
                if "t" in parts:
                    pe.wait_ge(q["t_p"], m + 2)
                    pe.wait_ge(q["t_ev"], m)
                    turn(pb[2 - s], el[:, s, :]).then_inc(q["t_tr"], 1)
                if "c" in parts:
                    pe.wait_ge(q["t_cs"], m)
                    pe.wait_ge(q["t_no"], m)
                    pe.transpose(bank_of(6 + s)[:, P:2 * P], cs[:, s, :], ident[:]).then_inc(q["t_ct"], 1)
                if "p" in parts:
                    pe.wait_ge(q["t_ev"], m + 1)
                    pe.wait_ge(q["t_x1"], m - 1)
                    weighted(bank_of(7 - s), 1 - s, b, 1).then_inc(q["t_pv"], 1)
                if "c" in parts:
                    pe.wait_ge(q["t_cc"], m)
                    product(bank_of(6 + s)[:, 2 * P:3 * P], csT[:, s, :], wcomb[:, b, :]).then_inc(q["t_xm"], 1)

            def rows_found(b):
                pe.wait_ge(q["k_good"], b + 1)
                pe.wait_ge(q["b_no"], TT + 2)
                product(bank_of(7)[0:1, 511:512], kfound[:], ones[:, 0:1]).then_inc(q["k_sum"], 1)

            def sparse_tail(b):
                stage(b, 0, 0, "t")
                stage(b, 1, 1, "tp")
                with pe.Fori(1, NT // 2) as i2:
                    for s in range(2):
                        stage(b, i2 * 2 + s, s)
                stage(b, NT, 0, "pc")
                stage(b, NT + 1, 1, "c")

            def second_norm(b):
                for t in range(NT):
                    pe.wait_ge(q["h_xh"], NT * b + t + 1)
                    pe.transpose(bank_of(t // TG)[:, t % TG * P:(t % TG + 1) * P], xhat[:, t % TG, :], ident[:]).then_inc(q["h_tr"], 1)
                for t in range(NT):
                    if t % TG == 0:
                        pe.wait_ge(q["h_hs"], NG * b + t // TG + 1)
                    last = product(bank_of(6)[:, t * E:(t + 1) * E], h2T[:, t * P:(t + 1) * P], gateWT[:])
                last.then_inc(q["h_lg"], 1)

            def expert(ex, up, down):
                for g in range(NG):
                    own = slice(g * GRP, (g + 1) * GRP)
                    for c in range(FC):
                        k = FC * g + c
                        pe.wait_ge(q["f_gu"], slot_freed(ex, k))
                        for j in range(2):
                            out = bank_of((gate_bank, up_bank)[j][k % 3])
                            high, low = (up(part, j)[:, c * P:(c + 1) * P] for part in range(2))
                            product(out, high, h2b[:, 0, own], True, False)
                            product(out, high, h2b[:, 1, own], False, False)
                            last = product(out, low, h2b[:, 0, own], False, True)
                        last.then_inc(q["f_up"], 1)
                for g in range(NG):
                    pe.wait_ge(q["f_gu"], ex * (NG * FC) + (FC * (g + 1) + 2))
                    pe.wait_ge(q["f_ac"], ex * (NG * TG) + TG * (g + 1))
                    for j in range(TG):
                        for c in range(FC):
                            last = product(bank_of(4 + g)[:, j * P:(j + 1) * P], gu[g][:, c, j * P:(j + 1) * P], down[:, c, :],
                                           c == 0, c == FC - 1)
                    last.then_inc(q["f_dn"], 1)

            def experts(b):
                pe.wait_ge(q["h_lo"], NG * (b + 1))
                pe.wait_ge(q["s_lo"], 1)
                pe.wait_ge(q["g_sub"], b + 1)
                expert((E + 1) * b, lambda part, j: w13sb[:, part, j, :], w2s)
                with pe.Fori(0, E // 2) as e2:
                    for s in range(2):
                        pe.wait_ge(q["w_lo"], e2 * 2 + (E * b + s + 1))
                        expert(e2 * 2 + (s + (E + 1) * b + 1), lambda part, j: w13b[:, s, part, j, :], w2[:, s, :, :])

            for b in range(B):
                rows_found(b)
                if b > 0:
                    pe.wait_ge(q["f_ac"], (E + 1) * NG * TG + 8)
                sparse_tail(b)
                second_norm(b)
                experts(b)


_INS = ['L0_attn_x', 'L0_attn_local_qkv_w', 'L0_attn_sparse_qkv_w', 'L0_attn_memory_bank', 'L0_attn_memory_proj_w',
        'L0_attn_mem_out_w', 'L0_attn_mem_out_b', 'L0_attn_pred_in_w', 'L0_attn_pred_in_b', 'L0_attn_pred1_w',
        'L0_attn_pred1_b', 'L0_attn_pred2_w', 'L0_attn_pred2_b', 'L0_attn_warboss_w', 'L0_attn_warboss_b',
        'L0_ffn_gate_W', 'L0_ffn_w1_e', 'L0_ffn_w3_e', 'L0_ffn_w2_e', 'L0_ffn_w1_s', 'L0_ffn_w3_s', 'L0_ffn_w2_s',
        'L0_c', 'L0_wmod']


def kernel(**inputs):
    import numpy as _np
    import concourse.bacc as _bacc
    from concourse import mybir as _mybir
    from concourse.bass_utils import run_bass_kernel_spmd as _run

    nc = _bacc.Bacc("TRN2", target_bir_lowering=False, num_devices=1)
    arrays, io = {}, {}
    for name in _INS:
        a = _np.ascontiguousarray(inputs[name])
        arrays[f"in_{name}_dram"] = a
        io[name] = nc.dram_tensor(f"in_{name}_dram", a.shape, _mybir.dt.from_np(a.dtype), kind="ExternalInput").ap()
    io["out"] = nc.dram_tensor("out_0_dram", inputs["L0_attn_x"].shape, _mybir.dt.float32, kind="ExternalOutput").ap()
    build(nc, io)
    r = _run(nc, [arrays], core_ids=[0])
    return r.results[0]["out_0_dram"]
```
